# Optimizing a Trainium2 kernel written in Bass

```python
import numpy as np
import jax
import jax.numpy as jnp

def _softmax(x, axis=-1):
    return jax.nn.softmax(x, axis=axis)

def _gelu(x):
    return jax.nn.gelu(x, approximate=True)

def _silu(x):
    return jax.nn.silu(x)

def _sigmoid(x):
    return jax.nn.sigmoid(x)

def _layernorm(x, axis=-1, eps=1e-05):
    m = jnp.mean(x, axis=axis, keepdims=True)
    v = jnp.var(x, axis=axis, keepdims=True)
    return (x - m) / jnp.sqrt(v + eps)

def _scatter_add(tgt, idx, src, axis=0):
    return tgt.at[idx].add(src)

def _segment_sum(src, seg, n):
    return jax.ops.segment_sum(src, seg, n)
kernel_name = 'mk_prb_d1_jaxref_r8_7a5701'

def setup_inputs(seed: int=0):
    np.random.seed(seed)
    _w = jnp.asarray

    def _L0_attn_setup():
        import jax, jax.numpy as jnp
        import numpy as np
        import math
        DIM = 128
        N_HEADS = 16
        HEAD_DIM = DIM // N_HEADS

        def get_sin_cos(seq_len, dim):
            theta = 10000.0 ** (-jnp.arange(0, dim, 2, dtype=jnp.float32) / dim)
            position = jnp.arange(seq_len, dtype=jnp.float32)
            freqs = position[:, None] * theta[None, :]
            emb = jnp.concatenate([jnp.sin(freqs), jnp.cos(freqs)], axis=-1)
            sin = emb[None, None]
            cos = emb[None, None]
            return (sin, cos)

        def rotate_half(x):
            x1, x2 = (x[..., ::2], x[..., 1::2])
            return jnp.concatenate([-x2, x1], axis=-1)

        def apply_rope(q, k):
            sin, cos = get_sin_cos(q.shape[2], q.shape[-1])
            q = q * cos + rotate_half(q) * sin
            k = k * cos + rotate_half(k) * sin
            return (q, k)
        key = jax.random.key(seed)
        ks = jax.random.split(key, 3)
        B, L, D = (2, 256, DIM)
        x = jax.random.normal(ks[0], (B, L, D), dtype=jnp.float32)
        Wqkv = jax.random.normal(ks[1], (D, 3 * D), dtype=jnp.float32) * (1.0 / math.sqrt(D))
        bqkv = jnp.zeros((3 * D,), dtype=jnp.float32)
        Wout = jax.random.normal(ks[2], (D, D), dtype=jnp.float32) * (1.0 / math.sqrt(D))
        bout = jnp.zeros((D,), dtype=jnp.float32)
        return {'x': x, 'Wqkv': Wqkv, 'bqkv': bqkv, 'Wout': Wout, 'bout': bout}
    _L0_attn_in = _L0_attn_setup()

    def _L0_ffn_setup():
        import jax, jax.numpy as jnp
        import numpy as np
        import math
        B, S, D = (4, 256, 128)
        E, DFF = (16, 256)
        CAP_FACTOR = 2.0
        ROUTER_HIDDEN = 128
        CAPACITY = int(math.ceil(S * CAP_FACTOR / E))
        key = jax.random.key(seed)
        ks = jax.random.split(key, 6)

        def uinit(k, shape, fan_in):
            bound = math.sqrt(3.0) * math.sqrt(1.0 / 3.0) / math.sqrt(fan_in)
            return jax.random.uniform(k, shape, jnp.float32, -bound, bound)
        return {'hidden_states': jax.random.normal(ks[0], (B, S, D), jnp.float32), 'router_w1': jax.random.normal(ks[1], (D, ROUTER_HIDDEN), jnp.float32) / math.sqrt(D), 'router_w2': jax.random.normal(ks[2], (ROUTER_HIDDEN, E), jnp.float32) / math.sqrt(ROUTER_HIDDEN), 'w1': uinit(ks[3], (E, D, DFF), D), 'w2': uinit(ks[4], (E, D, DFF), D), 'w3': uinit(ks[5], (E, DFF, D), DFF)}
    _L0_ffn_in = _L0_ffn_setup()
    _d = {'L0_attn_x': _L0_attn_in['x'], 'L0_attn_Wqkv': _L0_attn_in['Wqkv'], 'L0_attn_bqkv': _L0_attn_in['bqkv'], 'L0_attn_Wout': _L0_attn_in['Wout'], 'L0_attn_bout': _L0_attn_in['bout'], 'L0_ffn_router_w1': _L0_ffn_in['router_w1'], 'L0_ffn_router_w2': _L0_ffn_in['router_w2'], 'L0_ffn_w1': _L0_ffn_in['w1'], 'L0_ffn_w2': _L0_ffn_in['w2'], 'L0_ffn_w3': _L0_ffn_in['w3']}
    _x0 = _d['L0_attn_x']
    _d['L0_attn_x'] = jax.random.normal(jax.random.fold_in(jax.random.key(seed), 1), (16, 512, 128), dtype=_x0.dtype)
    del _x0
    return _d

def reference(L0_attn_x, L0_attn_Wqkv, L0_attn_bqkv, L0_attn_Wout, L0_attn_bout, L0_ffn_router_w1, L0_ffn_router_w2, L0_ffn_w1, L0_ffn_w2, L0_ffn_w3):

    def _L0_attn_ref(x, Wqkv, bqkv, Wout, bout):
        import jax, jax.numpy as jnp
        import numpy as np
        import math
        DIM = 128
        N_HEADS = 16
        HEAD_DIM = DIM // N_HEADS

        def get_sin_cos(seq_len, dim):
            theta = 10000.0 ** (-jnp.arange(0, dim, 2, dtype=jnp.float32) / dim)
            position = jnp.arange(seq_len, dtype=jnp.float32)
            freqs = position[:, None] * theta[None, :]
            emb = jnp.concatenate([jnp.sin(freqs), jnp.cos(freqs)], axis=-1)
            sin = emb[None, None]
            cos = emb[None, None]
            return (sin, cos)

        def rotate_half(x):
            x1, x2 = (x[..., ::2], x[..., 1::2])
            return jnp.concatenate([-x2, x1], axis=-1)

        def apply_rope(q, k):
            sin, cos = get_sin_cos(q.shape[2], q.shape[-1])
            q = q * cos + rotate_half(q) * sin
            k = k * cos + rotate_half(k) * sin
            return (q, k)
        B, L, D = x.shape
        H, Hd = (N_HEADS, HEAD_DIM)
        qkv = (x @ Wqkv + bqkv).reshape(B, L, 3, H, Hd)
        q, k, v = (qkv[:, :, 0], qkv[:, :, 1], qkv[:, :, 2])
        q = q.transpose(0, 2, 1, 3)
        k = k.transpose(0, 2, 1, 3)
        v = v.transpose(0, 2, 1, 3)
        q, k = apply_rope(q, k)
        scores = jnp.einsum('bhqd,bhkd->bhqk', q, k) / math.sqrt(Hd)
        probs = jax.nn.softmax(scores, axis=-1)
        out = jnp.einsum('bhqk,bhkd->bhqd', probs, v)
        out = out.transpose(0, 2, 1, 3).reshape(B, L, D)
        return out @ Wout + bout

    def _L0_ffn_ref(hidden_states, router_w1, router_w2, w1, w2, w3):
        import jax, jax.numpy as jnp
        import numpy as np
        import math
        B, S, D = (4, 256, 128)
        E, DFF = (16, 256)
        CAP_FACTOR = 2.0
        ROUTER_HIDDEN = 128
        CAPACITY = int(math.ceil(S * CAP_FACTOR / E))
        b, s, d = hidden_states.shape
        e = w1.shape[0]
        cap = CAPACITY
        router_logits = jax.nn.silu(hidden_states @ router_w1) @ router_w2
        expert_probs = jax.nn.softmax(router_logits.transpose(0, 2, 1), axis=-1)
        expert_weights, token_indices = jax.lax.top_k(expert_probs, cap)
        expert_weights = expert_weights / (expert_weights.sum(-1, keepdims=True) + 1e-09)
        expert_inputs = jax.vmap(lambda h, i: h[i])(hidden_states, token_indices)
        gate = jax.nn.silu(jnp.einsum('becd,edf->becf', expert_inputs, w1))
        value = jnp.einsum('becd,edf->becf', expert_inputs, w2)
        expert_out = jnp.einsum('becf,efd->becd', gate * value, w3)
        weighted = expert_out * expert_weights[..., None]

        def combine(idx, vals):
            return jnp.zeros((s, d), vals.dtype).at[idx.reshape(-1)].add(vals.reshape(-1, d))
        output = jax.vmap(combine)(token_indices, weighted)
        return output
    x = L0_attn_x
    xn = _layernorm(x, axis=-1)
    x = x + _L0_attn_ref(xn, L0_attn_Wqkv, L0_attn_bqkv, L0_attn_Wout, L0_attn_bout) + _L0_ffn_ref(xn, L0_ffn_router_w1, L0_ffn_router_w2, L0_ffn_w1, L0_ffn_w2, L0_ffn_w3)
    return x

_drawn_inputs = setup_inputs


def setup_inputs(seed=0):
    import zlib

    import numpy as np

    out = dict(_drawn_inputs(seed))
    spreads = {'L0_attn_bqkv': (0.0, 0.8), 'L0_attn_bout': (0.0, 0.8)}
    factors = {'L0_ffn_router_w1': 8.0,
     'L0_ffn_router_w2': 8.0,
     'L0_ffn_w1': 8.0,
     'L0_ffn_w2': 8.0,
     'L0_ffn_w3': 8.0,
     'L0_attn_Wqkv': 5.242,
     'L0_attn_Wout': 4.073}
    for name, (base, spread) in spreads.items():
        noise = np.random.default_rng([zlib.crc32(name.encode()), seed]).standard_normal(out[name].shape)
        drawn = base * np.exp(spread * noise) if base else spread * noise
        out[name] = jnp.asarray(drawn.astype(out[name].dtype))
    for name, factor in factors.items():
        out[name] = (out[name] * factor).astype(out[name].dtype)
    return out
```

```python
from collections import namedtuple
from contextlib import ExitStack

import numpy as np

import concourse.bass as bass
from concourse import mybir

F32 = mybir.dt.float32
BF16 = mybir.dt.bfloat16
I32 = mybir.dt.int32
U32 = mybir.dt.uint32
ALU = mybir.AluOpType
ACT = mybir.ActivationFunctionType
AX_X = mybir.AxisListType.X

P = 128
HEADS = 16
HD = 8
CAP = 32
LN_EPS = 1e-5
W_EPS = 1e-9
DMA = 16

G = 4
KB = 4
Q_PARTS = (0, 1, 2, 0, 1, 0)
K_PARTS = (0, 0, 0, 1, 1, 2)
SCORE_ROWS = 96
STACK_ROWS = 98

TASK_AT = {0: "c0", 1: "q", 2: "k", 3: "v", 4: "c1", 5: "xe", 6: "gate0", 7: "value0", 8: "c2", 9: "o",
           10: "gate1", 11: "value1", 12: "c3", 13: "y"}
PROLOGUE = ["bias", "q", "k", "v", "c", "route"]
Batch = namedtuple("Batch", "n par first last")


def constants(S):
    theta = (10000.0 ** (-np.arange(0, HD, 2, dtype=np.float32) / HD)).astype(np.float32)
    freqs = np.arange(S, dtype=np.float32)[:, None] * theta[None, :]
    emb = np.concatenate([np.sin(freqs), np.cos(freqs)], axis=-1).astype(np.float32)
    table = np.zeros((P, S + P + 2), np.float32)
    table[:, :S] = np.repeat(emb.T, HEADS, axis=0)
    table[:, S:S + P] = np.eye(P, dtype=np.float32)
    for t in range(2):
        table[:, S + P + t] = S * (8 * t + np.arange(P) // 16)
    return table


def attention_and_experts(nc, x, Wqkv, bqkv, Wout, bout, rw1, rw2, w1, w2, w3, table, fill, out):
    B, S, D = x.shape
    E, _, FF = w1.shape
    T = S // P
    NF = FF // P
    assert (D, S, T, E, B, NF) == (P, 512, KB, 16, 16, 2)
    SCALE = float(HD) ** -0.5

    rows = x.rearrange("b s d -> (b s) d")
    out_rows = out.rearrange("b s d -> (b s) d")
    xn_rows = nc.dram_tensor("xn_rows", (B * S, D), F32).ap()
    xT_dram = nc.dram_tensor("xT_dram", (B * P, S), F32).ap()
    logits_dram = nc.dram_tensor("logits_dram", (B * E, S), F32).ap()
    split_dram = nc.dram_tensor("split_dram", (2, 2, 3, P, S), BF16).ap()
    o_dram = nc.dram_tensor("o_dram", (2, HEADS, HD + 1, S), F32).ap()
    rden_dram = nc.dram_tensor("rden_dram", (2, HEADS, S), F32).ap()

    with ExitStack() as ctx:
        def sb(name, shape, dt=F32):
            return ctx.enter_context(nc.sbuf_tensor(name, shape, dt))

        def sem(name):
            return ctx.enter_context(nc.semaphore(name))

        consts = sb("consts", [P, S + P + 2])
        emb = consts[:, 0:S]
        ident = consts[:, S:S + P]
        row_base = consts[:, S + P:S + P + 2]
        wqkv = sb("wqkv", [P, 3 * D])
        wqk = sb("wqk", [P, 2, D])
        wo = sb("wo", [P, D])
        rw1_sb = sb("rw1_sb", [P, P])
        rw2_sb = sb("rw2_sb", [P, E])
        bias_row = sb("bias_row", [1, 3 * D])
        bqk_row = sb("bqk_row", [1, 2, D])
        one = sb("one", [1, 1])
        bqk = sb("bqk", [P, 2])
        bv_all = sb("bv_all", [P, D])
        bout_all = sb("bout_all", [P, D])

        xt = sb("xt", [P, 2, T, D])
        xn = sb("xn", [P, 2, T, D])
        xb = sb("xb", [P, 2, T, D])
        xT = sb("xT", [P, 2, S])
        stats = sb("stats", [P, T, 6])
        mean = sb("mean", [P, T])
        apart = sb("apart", [P, T])
        var_in = sb("var_in", [P, T])
        pace = sb("pace", [P, 1])
        var_eps = sb("var_eps", [P, T])
        minus_half = sb("minus_half", [P, T])
        rstd = sb("rstd", [P, T])
        rt = sb("rt", [P, 2, S])
        rh = sb("rh", [P, 2, S])
        lg = sb("lg", [E, 2, S])

        probs = sb("probs", [P, 2, S])
        rmax = sb("rmax", [P, 2])
        zsum = sb("zsum", [P, 2])
        rz = sb("rz", [P, 2])
        vals = sb("vals", [P, 2, CAP])
        idx = sb("idx", [P, 2, CAP], U32)
        route_in = sb("route_in", [P, 4, CAP])
        idx_all = sb("idx_all", [P, E * T], I32)
        w_all = sb("w_all", [P, E * T])
        idx_now = sb("idx_now", [P, 2, T], I32)

        q_stack = sb("q_stack", [P, 2, HEADS, S], BF16)
        k_stack = sb("k_stack", [P, 2, HEADS, S], BF16)
        full = sb("full", [P, 2, S])
        rest = sb("rest", [P, 2, S])
        split = sb("split", [P, 2, 3, S], BF16)
        v_ones = sb("v_ones", [P, 2, KB, HEADS, 32])
        mx = sb("mx", [P, 2, 16])
        cmax = sb("cmax", [16, 2, 2, P], BF16)
        probsT = sb("probsT", [P, 8, S])
        oT = sb("oT", [P, 2, S])
        num = sb("num", [P, S])
        den = sb("den", [P, S // 8])
        rden = sb("rden", [P, S // 8])
        rden_all = sb("rden_all", [P, S])
        onorm = sb("onorm", [P, S])
        att = sb("att", [P, T, D])

        w12 = sb("w12", [P, 2, 2, FF])
        w3_sb = sb("w3_sb", [P, 2, NF, D])
        xg = sb("xg", [P, 2, T, D])
        xe = sb("xe", [P, S])
        th = sb("th", [P, S])
        gated = sb("gated", [P, S])
        hT = sb("hT", [P, NF, S])
        ys = sb("ys", [P, T, D])

        psum = ctx.enter_context(nc.psum_tensor("psum", [P, 8, 512], F32))
        SM, ST, PV, MISC = (0, 1, 2), (3, 4, 5), 6, 7
        misc = psum[:, MISC, :]

        consts_in = sem("consts_in")
        weights_in = sem("weights_in")
        ones_set = sem("ones_set")
        v_ones_set = sem("v_ones_set")
        half_set = sem("half_set")
        paced = sem("paced")
        fill_in = sem("fill_in")
        wqk_made = sem("wqk_made")
        x_in = [sem("x_in0"), sem("x_in1")]
        ln_step = sem("ln_step")
        var_made = sem("var_made")
        rstd_made = sem("rstd_made")
        xn_made = sem("xn_made")
        xb_made = sem("xb_made")
        xT_done = sem("xT_done")
        xT_made = sem("xT_made")
        hid_done = sem("hid_done")
        rt_made = sem("rt_made")
        rh_made = sem("rh_made")
        lg_done = sem("lg_done")
        lg_made = sem("lg_made")
        xn_out = [sem("xn_out0"), sem("xn_out1")]
        xT_out = [sem("xT_out0"), sem("xT_out1")]
        lg_out = [sem("lg_out0"), sem("lg_out1")]
        xb_out = [sem("xb_out0"), sem("xb_out1")]

        lg_in = sem("lg_in")
        route_step = sem("route_step")
        exp_made = sem("exp_made")
        idx_copied = sem("idx_copied")

        xT_in = [sem("xT_in0"), sem("xT_in1")]
        w_in = [sem("w_in0"), sem("w_in1")]
        cast_done = sem("cast_done")
        sub_done = sem("sub_done")
        split_out = sem("split_out")
        stacks_in = sem("stacks_in")
        sm_done = sem("sm_done")
        max_done = sem("max_done")
        chi_made = sem("chi_made")
        cmax_in = sem("cmax_in")
        st_done = sem("st_done")
        exp_done = sem("exp_done")
        pv_done = sem("pv_done")
        oT_made = sem("oT_made")
        oT_out = [sem("oT_out0"), sem("oT_out1")]
        num_in = sem("num_in")
        den_in = sem("den_in")
        rden_made = sem("rden_made")
        rden_out = sem("rden_out")
        rden_in = sem("rden_in")
        norm_made = sem("norm_made")
        misc_done = sem("misc_done")
        misc_free = sem("misc_free")
        th_made = sem("th_made")
        gathered = [sem("gathered0"), sem("gathered1")]
        added = sem("added")

        def after(eng, semaphore, count):
            if not (isinstance(count, int) and count <= 0):
                eng.wait_ge(semaphore, count)

        def through(b, par, per=DMA):
            return (b - par) * (per // 2) + per

        def before(b, par, per=DMA):
            return (b - par) * (per // 2)

        def ring(g, i, j):
            k = 16 * g + 4 * i + j
            return (k % 3 if k < 62 else (0, 2)[k - 62]), {62: 2, 63: 4, 0: 2, 1: 4}.get(k, 3)

        def after_all(eng, semaphores, count):
            for semaphore in semaphores:
                eng.wait_ge(semaphore, count)

        def tasks(bt):
            names = list(TASK_AT.values())
            if bt.first:
                names.remove("o")
            if bt.last:
                names = [n for n in names if n not in ("q", "k", "v", "c3")]
            return names

        def task_no(bt, name):
            if bt is None:
                return PROLOGUE.index(name)
            start = len(PROLOGUE) if bt.first else len(PROLOGUE) + len(TASK_AT) * bt.n - 1
            return start + tasks(bt).index(name)

        def batches(eng, body):
            body(Batch(0, 0, True, False))
            body(Batch(1, 1, False, False))
            with eng.Fori(1, B // 2 - 1) as i:
                body(Batch(2 * i, 0, False, False))
                body(Batch(2 * i + 1, 1, False, False))
            body(Batch(B - 2, 0, False, False))
            body(Batch(B - 1, 1, False, True))

        def phase1(eng, body):
            body(0, 0, True)
            body(1, 1, False)
            with eng.Fori(1, B // 2) as i:
                body(2 * i, 0, False)
                body(2 * i + 1, 1, False)

        block = ctx.enter_context(nc.Block())
        N_CONSTS, N_WEIGHTS = 4, 3 + HD

        @block.sync
        def _(sp):
            def load_x(b, par):
                after(sp, xn_made, b - 1)
                after(sp, xb_made, b - 1)
                sp.dma_start(xt[:, par], rows[bass.ds(b * S, S), :].rearrange("(t p) d -> p t d", p=P)
                             ).then_inc(x_in[par], DMA)

            load_x(0, 0)
            sp.dma_start(consts[:], table).then_inc(consts_in, DMA)
            sp.dma_start(rw1_sb[:], rw1).then_inc(consts_in, DMA)
            sp.dma_start(rw2_sb[:], rw2).then_inc(consts_in, DMA)
            sp.dma_start(bout_all[:], bout.rearrange("(a d) -> a d", a=1).broadcast_to([P, D])).then_inc(consts_in, DMA)
            load_x(1, 1)
            sp.dma_start(wqkv[:], Wqkv).then_inc(weights_in, DMA)
            sp.dma_start(bias_row[:], bqkv.rearrange("(a d) -> a d", a=1)).then_inc(weights_in, DMA)
            sp.dma_start(bv_all[:], bqkv[2 * D:3 * D].rearrange("(a d) -> a d", a=1).broadcast_to([P, D])
                         ).then_inc(weights_in, DMA)
            for d in range(HD):
                sp.dma_start(wo[HEADS * d:HEADS * (d + 1), :], Wout.rearrange("(h d) n -> d h n", d=HD)[d]
                             ).then_inc(weights_in, DMA)
            unused = SCORE_ROWS - 8 * len(Q_PARTS)
            for a in range(2):
                for stack in (q_stack, k_stack):
                    sp.dma_start(stack[SCORE_ROWS - unused:SCORE_ROWS, a].rearrange("p h s -> p (h s)"),
                                 fill[0:1, :].broadcast_to([unused, HEADS * S])).then_inc(fill_in, DMA)
            sp.dma_start(k_stack[SCORE_ROWS:STACK_ROWS].rearrange("p a h s -> p (a h s)"),
                         fill[1:3, :].rearrange("a n -> (a n)").rearrange("(a n) -> a n", a=1).broadcast_to(
                             [2, 2 * HEADS * S])).then_inc(fill_in, DMA)
            for n, w in enumerate((w1, w2)):
                sp.dma_start(w12[:, 0, n, :], w[0]).then_inc(w_in[0], DMA)
            sp.dma_start(w3_sb[:, 0], w3[0].rearrange("(f p) d -> p f d", p=P)).then_inc(w_in[0], DMA)

            def loads(b, par, first):
                load_x(b, par)

            with sp.Fori(1, B // 2) as i:
                load_x(2 * i, 0)
                load_x(2 * i + 1, 1)

            after_all(sp, lg_out, DMA * B // 2)
            sp.dma_start(probs[:], logits_dram.rearrange("(t p) s -> p t s", p=P)).then_inc(lg_in, DMA)

            def load_xT(b, par):
                after_all(sp, xT_out, DMA * B // 2)
                sp.dma_start(xT[:, par], xT_dram[bass.ds(b * P, P), :]).then_inc(xT_in[par], DMA)

            after(sp, hid_done, B)
            load_xT(0, 0)
            load_xT(1, 1)

            def fill_stacks(b, par):
                after(sp, stacks_in, 6 * DMA * (b - 1))
                after(sp, sub_done, 4 * b + 3)
                sp.dma_start(split_dram[par, 0].rearrange("q p s -> p q s"), split[:, 0]).then_inc(split_out, DMA)
                after(sp, sub_done, 4 * b + 4)
                sp.dma_start(split_dram[par, 1].rearrange("q p s -> p q s"), split[:, 1]).then_inc(split_out, DMA)
                after(sp, split_out, 2 * DMA * b + 2 * DMA)
                at = 0
                for part, n in enumerate((3, 2, 1)):
                    sp.dma_start(q_stack[at:at + 8 * n, par], split_dram[par, 0, 0:n].rearrange(
                        "q (d h) s -> (q d) h s", h=HEADS)).then_inc(stacks_in, DMA)
                    sp.dma_start(k_stack[at:at + 8 * n, par], split_dram[par, 1, part:part + 1].rearrange(
                        "q (d h) s -> q d h s", h=HEADS).broadcast_to([n, HD, HEADS, S])).then_inc(stacks_in, DMA)
                    at += 8 * n

            def move_cmax(v, par, gg, task):
                cp = gg % 2
                after(sp, misc_free, task + 1)
                after(sp, st_done, 16 * (v - 7))
                for r in range(2):
                    sp.dma_start(q_stack[SCORE_ROWS + r:SCORE_ROWS + r + 1, par, G * gg:G * gg + G, :].rearrange(
                        "r h (b q) -> r (h b) q", b=KB), cmax[:, cp, r, :]).then_inc(cmax_in, DMA)

            def store_oT(b, par, g):
                after(sp, oT_made, 4 * b + g + 1)
                for j in range(G):
                    sp.dma_start(o_dram[par, G * g + j], oT[32 * j:32 * j + HD + 1, g % 2, :]
                                 ).then_inc(oT_out[g % 2], DMA)

            def load_den(b, par):
                after_all(sp, oT_out, 2 * G * DMA * (b + 1))
                after(sp, rden_made, b)
                sp.dma_start(den[:], o_dram[par, :, HD].rearrange("h (c s) -> h c s", c=8)).then_inc(den_in, DMA)
                after(sp, norm_made, b)
                sp.dma_start(num[:], o_dram[par, :, 0:HD].rearrange("h d s -> d h s")).then_inc(num_in, DMA)

            def store_rden(b, par):
                after(sp, rden_made, b + 1)
                sp.dma_start(rden_dram[par].rearrange("h (c s) -> (h c) s", c=8), rden[:]).then_inc(rden_out, DMA)

            def spread_rden(b, par):
                after(sp, rden_out, DMA * (b + 1))
                sp.dma_start(rden_all[:], rden_dram[par:par + 1].broadcast_to([HD, HEADS, S])).then_inc(rden_in, DMA)

            fill_stacks(0, 0)
            move_cmax(0, 0, 0, task_no(None, "c"))

            def body(bt):
                b, par = bt.n, bt.par
                if not bt.last:
                    if not bt.first:
                        prev = task_no(Batch(b, par, False, False), "c0") - 1
                        after(sp, misc_done, prev + 1)
                    for n, w in enumerate((w1, w2)):
                        sp.dma_start(w12[:, 1 - par, n, :], w.rearrange("e p f -> (e p) f")[bass.ds((b + 1) * P, P), :]
                                     ).then_inc(w_in[1 - par], DMA)
                    sp.dma_start(w3_sb[:, 1 - par], w3.rearrange("e f d -> (e f) d")[bass.ds((b + 1) * FF, FF), :]
                                 .rearrange("(f p) d -> p f d", p=P)).then_inc(w_in[1 - par], DMA)
                for g in range(4):
                    if not (bt.last and g == 3):
                        v, vpar = (4 * b + g + 1, par if g < 3 else 1 - par)
                        move_cmax(v, vpar, (g + 1) % 4, task_no(bt, f"c{g}"))
                    if not (bt.first and g == 0):
                        if g == 1 and not bt.first:
                            spread_rden(b - 1, 1 - par)
                        if g:
                            store_oT(b, par, g - 1)
                        else:
                            store_oT(b - 1, 1 - par, 3)
                            load_den(b - 1, 1 - par)
                    if g == 0 and not bt.last:
                        fill_stacks(b + 1, 1 - par)
                        if not (isinstance(b, int) and b + 2 >= B):
                            after(sp, misc_done, task_no(bt, "c0"))
                            load_xT(b + 2, par)
                    if g == 0 and not bt.first:
                        store_rden(b - 1, 1 - par)

            batches(sp, body)
            store_oT(B - 1, 1, 3)
            load_den(B - 1, 1)
            store_rden(B - 1, 1)
            spread_rden(B - 1, 1)

        @block.tensor
        def _(pe):
            pe.wait_ge(consts_in, DMA * N_CONSTS)

            def logits(b, par):
                pe.wait_ge(rh_made, b + 1)
                after(pe, lg_made, b - 1)
                nc.tensor.matmul(psum[0:E, 4 + par, :], rw2_sb[:], rh[:, par], start=True, stop=True
                                 ).then_inc(lg_done, 1)

            def route_body(b, par, first):
                pe.wait_ge(xn_made, b + 1)
                after(pe, xT_made, b - 1)
                for t in range(T):
                    last = nc.tensor.transpose(psum[:, par, t * P:(t + 1) * P], xn[:, par, t, :], ident)
                last.then_inc(xT_done, 1)
                if not first:
                    logits(b - 1, 1 - par)
                pe.wait_ge(xT_made, b + 1)
                after(pe, rh_made, b - 1)
                nc.tensor.matmul(psum[:, 2 + par, :], rw1_sb[:], xT[:, par], start=True, stop=True
                                 ).then_inc(hid_done, 1)

            phase1(pe, route_body)
            logits(B - 1, 1)
            pe.wait_ge(lg_made, B)

            def start_task(no):
                after(pe, misc_free, no)

            def project_qk(no, b, par, n):
                if n == 0:
                    pe.wait_ge(xT_in[par], through(b, par))
                start_task(no)
                nc.tensor.matmul(misc, wqk[:, n, :], xT[:, par], start=True, stop=True).then_inc(misc_done, 1)

            def project_v(no, par):
                start_task(no)
                for t in range(T):
                    last = nc.tensor.matmul(misc[:, t * P:(t + 1) * P], xT[:, par, t * P:(t + 1) * P],
                                            wqkv[:, 2 * D:3 * D], start=True, stop=True)
                last.then_inc(misc_done, 1)

            def transpose_max(no, v, gp):
                pe.wait_ge(max_done, 16 * v + 16)
                start_task(no)
                nc.tensor.transpose(misc[0:16, 0:P], mx[:, gp, :], ident).then_inc(misc_done, 1)

            def score_for_max(b, par, g, i, j):
                n = 64 * b + 16 * g + 4 * i + j
                if (g, i, j) == (0, 0, 0):
                    pe.wait_ge(stacks_in, 6 * DMA * b + 6 * DMA)
                bank, ago = ring(g, i, j)
                after(pe, max_done, n - ago + 1)
                h = G * g + i
                nc.tensor.matmul(psum[:, SM[bank], :], q_stack[0:SCORE_ROWS, par, h, j * P:(j + 1) * P],
                                 k_stack[0:SCORE_ROWS, par, h, :], start=True, stop=True).then_inc(sm_done, 1)

            def score_for_exp(b, par, g, i, j):
                m = 64 * b + 16 * g + 4 * i + j
                if (i, j) == (0, 0):
                    pe.wait_ge(cmax_in, 2 * DMA * (4 * b + g) + 2 * DMA)
                bank, ago = ring(g, i, j)
                after(pe, exp_done, m - ago + 1)
                h = G * g + j
                nc.tensor.matmul(psum[:, ST[bank], :], k_stack[0:STACK_ROWS, par, h, i * P:(i + 1) * P],
                                 q_stack[0:STACK_ROWS, par, h, :], start=True, stop=True).then_inc(st_done, 1)

            def times_v(b, par, g, i, v_task):
                step = 16 * b + 4 * g + i
                pe.wait_ge(exp_done, 4 * step + 4)
                if (g, i) == (0, 0):
                    pe.wait_ge(misc_free, v_task + 1)
                if i == 0:
                    after(pe, oT_made, 4 * b + g)
                for j in range(G):
                    last = nc.tensor.matmul(psum[32 * j:32 * j + 32, PV, :], v_ones[:, par, i, G * g + j, :],
                                            probsT[:, 4 * (i % 2) + j, :], start=(i == 0), stop=(i == KB - 1))
                last.then_inc(pv_done, 1)

            def project_out(no, b):
                pe.wait_ge(norm_made, b + 1)
                start_task(no)
                for t in range(T):
                    last = nc.tensor.matmul(misc[:, t * P:(t + 1) * P], onorm[:, t * P:(t + 1) * P], wo[:],
                                            start=True, stop=True)
                last.then_inc(misc_done, 1)

            pe.wait_ge(weights_in, DMA * N_WEIGHTS)
            pe.wait_ge(wqk_made, 2)
            for n in range(2):
                last = nc.tensor.matmul(misc[:, n:n + 1], bqk_row[0:1, n, :], one[0:1, 0:1], start=True, stop=True)
            last.then_inc(misc_done, 1)
            project_qk(1, 0, 0, 0)
            project_qk(2, 0, 0, 1)
            project_v(3, 0)
            pe.wait_ge(fill_in, 5 * DMA)
            pe.wait_ge(v_ones_set, 1)
            for g in range(2):
                for i in range(4):
                    for j in range(4):
                        score_for_max(0, 0, g, i, j)
                if g == 0:
                    transpose_max(4, 0, 0)
            pe.wait_ge(route_step, ROUTE_STEPS)
            start_task(5)
            for n in range(4):
                last = nc.tensor.transpose(misc[0:CAP, n * P:(n + 1) * P], route_in[:, n, :], ident)
            last.then_inc(misc_done, 1)

            def body(bt):
                b, par = bt.n, bt.par
                for s in range(16):
                    g, i = divmod(s, 4)
                    for j in range(4):
                        if g < 2:
                            score_for_max(b, par, g + 2, i, j)
                        elif not bt.last:
                            score_for_max(b + 1, 1 - par, g - 2, i, j)
                        score_for_exp(b, par, g, i, j)
                        if j == 1 and s:
                            times_v(b, par, (s - 1) // 4, (s - 1) % 4,
                                    task_no(None, "v") if bt.first else v_task_of_prev(bt))
                        elif j == 1 and not bt.first:
                            times_v(b - 1, 1 - par, 3, 3, None)
                    name = TASK_AT.get(s)
                    if name not in tasks(bt):
                        continue
                    no = task_no(bt, name)
                    if name[0] == "c":
                        transpose_max(no, 4 * b + g + 1, (g + 1) % 2)
                    elif name in ("q", "k"):
                        project_qk(no, b + 1, 1 - par, "qk".index(name))
                    elif name == "v":
                        project_v(no, 1 - par)
                    elif name == "o":
                        project_out(no, b - 1)
                    elif name == "xe":
                        pe.wait_ge(gathered[par], through(b, par, T * DMA))
                        start_task(no)
                        for t in range(T):
                            last = nc.tensor.transpose(misc[:, t * P:(t + 1) * P], xg[:, par, t, :], ident)
                        last.then_inc(misc_done, 1)
                    elif name[:-1] in ("gate", "value"):
                        n, f = (0 if name[0] == "g" else 1), int(name[-1])
                        if (n, f) == (0, 0):
                            pe.wait_ge(w_in[par], through(b, par, 3 * DMA))
                        start_task(no)
                        nc.tensor.matmul(misc, w12[:, par, n, f * P:(f + 1) * P], xe[:], start=True, stop=True
                                         ).then_inc(misc_done, 1)
                    elif name == "y":
                        start_task(no)
                        for t in range(T):
                            for f in range(NF):
                                last = nc.tensor.matmul(misc[:, t * P:(t + 1) * P], hT[:, f, t * P:(t + 1) * P],
                                                        w3_sb[:, par, f, :], start=(f == 0), stop=(f == NF - 1))
                        last.then_inc(misc_done, 1)

            batches(pe, body)
            times_v(B - 1, 1, 3, 3, None)
            project_out(task_no(Batch(B - 1, 1, False, True), "y") + 1, B - 1)

        @block.scalar
        def _(act):
            def router_out(b, par):
                act.wait_ge(lg_done, b + 1)
                after(act, lg_out[par], before(b, par))
                nc.scalar.mul(lg[:, par], psum[0:E, 4 + par, :], 0.5).then_inc(lg_made, 1)
                act.wait_ge(lg_made, b + 1)
                act.dma_start(logits_dram[bass.ds(b * E, E), :], lg[:, par]).then_inc(lg_out[par], DMA)

            def route_body(b, par, first):
                act.wait_ge(xT_done, b + 1)
                after(act, xT_out[par], before(b, par))
                after(act, hid_done, b - 1)
                nc.scalar.copy(xT[:, par], psum[:, par, :]).then_inc(xT_made, 1)
                act.wait_ge(xn_made, b + 1)
                act.dma_start(xn_rows[bass.ds(b * S, S), :].rearrange("(t p) d -> p t d", p=P), xn[:, par]
                              ).then_inc(xn_out[par], DMA)
                act.wait_ge(xT_made, b + 1)
                act.dma_start(xT_dram[bass.ds(b * P, P), :], xT[:, par]).then_inc(xT_out[par], DMA)
                act.wait_ge(hid_done, b + 1)
                after(act, rh_made, b - 1)
                nc.scalar.activation(rt[:, par], psum[:, 2 + par, :], ACT.Tanh, scale=0.5).then_inc(rt_made, 1)
                if not first:
                    router_out(b - 1, 1 - par)

            phase1(act, route_body)
            router_out(B - 1, 1)

            def high_part(no, v, gp):
                act.wait_ge(misc_done, no + 1)
                after(act, cmax_in, 2 * DMA * (v - 1))
                nc.scalar.mul(cmax[:, gp, 0, :], misc[0:16, 0:P], -1.0).then_inc(chi_made, 1)

            high_part(4, 0, 0)
            for t in range(2):
                act.wait_ge(route_step, 2 * t + 2)
                nc.scalar.activation(probs[:, t, :], probs[:, t, :], ACT.Exp, bias=rmax[:, t:t + 1],
                                     accum_out=zsum[:, t:t + 1]).then_inc(exp_made, 1)

            def save_oT(b, g):
                act.wait_ge(pv_done, 16 * b + 4 * g + 4)
                after(act, oT_out[g % 2], G * DMA * (2 * b + g // 2))
                nc.scalar.copy(oT[:, g % 2], psum[:, PV, :]).then_inc(oT_made, 1)

            def body(bt):
                b, par = bt.n, bt.par
                for s in range(16):
                    g, i = divmod(s, 4)
                    for j in range(4):
                        m = 64 * b + 4 * s + j
                        act.wait_ge(st_done, m + 1)
                        if j == 0:
                            after(act, pv_done, 16 * b + s - 1)
                        nc.scalar.activation(probsT[:, 4 * (i % 2) + j, :], psum[:, ST[ring(g, i, j)[0]], :], ACT.Exp, scale=SCALE
                                             ).then_inc(exp_done, 1)
                        if j == 0:
                            task(bt, s - 1)
                        if j == 2 and i == 0 and not (bt.first and g == 0):
                            save_oT(b if g else b - 1, (g - 1) % 4)

            def task(bt, s):
                b, g = bt.n, s // 4
                name = TASK_AT.get(s)
                if name not in tasks(bt):
                    return
                no = task_no(bt, name)
                if name[0] == "c":
                    high_part(no, 4 * b + g + 1, (g + 1) % 2)
                elif name == "xe":
                    act.wait_ge(misc_done, no + 1)
                    nc.scalar.copy(xe[:], misc).then_inc(misc_free, 1)
                elif name == "o":
                    act.wait_ge(misc_done, no + 1)
                    after(act, added, DMA * 5 * (b - 1))
                    nc.scalar.copy(att[:].rearrange("p t d -> p (t d)"), misc).then_inc(misc_free, 1)
                elif name[0] == "g":
                    act.wait_ge(misc_done, no + 1)
                    nc.scalar.activation(th[:], misc, ACT.Tanh, scale=0.5).then_inc(th_made, 1)

            batches(act, body)
            save_oT(B - 1, 3)
            no = task_no(Batch(B - 1, 1, False, True), "y") + 1
            act.wait_ge(misc_done, no + 1)
            act.wait_ge(added, DMA * 5 * (B - 1))
            nc.scalar.copy(att[:].rearrange("p t d -> p (t d)"), misc).then_inc(misc_free, 1)

        @block.vector
        def _(dve):
            nc.vector.memset(one[:], 1.0).then_inc(ones_set, 1)
            nc.vector.memset(v_ones[:].rearrange("p a k h c -> p (a k h c)"), 1.0).then_inc(v_ones_set, 1)

            def hidden(b, par):
                dve.wait_ge(rt_made, b + 1)
                after(dve, lg_done, b - 1)
                nc.vector.scalar_tensor_tensor(rh[:, par], rt[:, par], 1.0, psum[:, 2 + par, :], ALU.add, ALU.mult
                                               ).then_inc(rh_made, 1)

            def route_body(b, par, first):
                dve.wait_ge(x_in[par], through(b, par))
                for t in range(T):
                    last = nc.vector.bn_stats(stats[:, t, :], xt[:, par, t, :])
                last.then_inc(ln_step, 1)
                dve.wait_ge(ln_step, 3 * b + 1)
                even, odd = stats[:, :, 0:3], stats[:, :, 3:6]
                nc.vector.tensor_tensor(mean[:], even[:, :, 1], odd[:, :, 1], ALU.add)
                nc.vector.tensor_tensor(apart[:], even[:, :, 1], odd[:, :, 1], ALU.subtract)
                nc.vector.tensor_tensor(var_eps[:], even[:, :, 2], odd[:, :, 2], ALU.add).then_inc(ln_step, 1)
                dve.wait_ge(ln_step, 3 * b + 2)
                nc.vector.tensor_scalar(mean[:], mean[:], 0.5, None, ALU.mult)
                nc.vector.scalar_tensor_tensor(apart[:], apart[:], 0.25, apart[:], ALU.mult, ALU.mult)
                nc.vector.tensor_scalar(var_in[:], var_eps[:], 1.0 / D, LN_EPS, ALU.mult, ALU.add
                                        ).then_inc(ln_step, 1)
                dve.wait_ge(ln_step, 3 * b + 3)
                nc.vector.tensor_tensor(var_eps[:], var_in[:], apart[:], ALU.add).then_inc(var_made, 1)
                dve.wait_ge(rstd_made, b + 1)
                after(dve, xn_out[par], before(b, par))
                after(dve, xT_done, b - 1)
                for t in range(T):
                    last = nc.vector.tensor_scalar(xn[:, par, t, :], xt[:, par, t, :], mean[:, t:t + 1],
                                                   rstd[:, t:t + 1], ALU.subtract, ALU.mult)
                last.then_inc(xn_made, 1)
                if not first:
                    hidden(b - 1, 1 - par)

            dve.wait_ge(weights_in, DMA * N_WEIGHTS)
            for src, dst, sm in ((wqkv, wqk, None), (bias_row, bqk_row, wqk_made)):
                v = src[:, 0:2 * D].rearrange("p (n h d) -> p n h d", n=2, h=HEADS)
                o = dst[:].rearrange("p n (d h) -> p n h d", d=HD)
                for n in range(2):
                    nc.vector.tensor_tensor(o[:, n, :, 0:4], v[:, n, :, 0:4], v[:, n, :, 1::2], ALU.subtract)
                    last = nc.vector.tensor_tensor(o[:, n, :, 4:8], v[:, n, :, 4:8], v[:, n, :, 0::2], ALU.add)
                last.then_inc(wqk_made, 1)

            phase1(dve, route_body)
            hidden(B - 1, 1)

            def scale_and_rotate(no, b, n):
                dve.wait_ge(misc_done, no + 1)
                after(dve, sub_done, 4 * (b - 1) + n + 1)
                nc.vector.scalar_tensor_tensor(full[:, n], misc, bqk[:, n:n + 1], emb, ALU.add, ALU.mult
                                               ).then_inc(misc_free, 1)
                dve.wait_ge(misc_free, no + 1)
                after(dve, split_out, 2 * DMA * b)
                nc.vector.tensor_copy(split[:, n, 0, :], full[:, n]).then_inc(cast_done, 1)

            def middle_part(b, n):
                dve.wait_ge(sub_done, 4 * b + n + 1)
                nc.vector.tensor_copy(split[:, n, 1, :], rest[:, n]).then_inc(cast_done, 1)

            def save_v(no, b, par):
                dve.wait_ge(misc_done, no + 1)
                after(dve, pv_done, 16 * (b - 1))
                nc.vector.tensor_tensor(
                    v_ones[:, par, :, :, 0:HD], misc.rearrange("p (k h d) -> p k h d", k=KB, h=HEADS),
                    bv_all[:].rearrange("p (a h d) -> p a h d", a=1, h=HEADS).broadcast_to([P, KB, HEADS, HD]),
                    ALU.add).then_inc(misc_free, 1)

            def maximum(b, g, i, j):
                n = 64 * b + 16 * g + 4 * i + j
                dve.wait_ge(sm_done, n + 1)
                nc.vector.tensor_reduce(mx[:, g % 2, 4 * i + j:4 * i + j + 1], psum[:, SM[ring(g, i, j)[0]], :], AX_X, ALU.max
                                        ).then_inc(max_done, 1)

            def low_part(no, v, gp):
                dve.wait_ge(chi_made, v + 1)
                nc.vector.scalar_tensor_tensor(cmax[:, gp, 1, :], misc[0:16, 0:P], -1.0, cmax[:, gp, 0, :],
                                               ALU.mult, ALU.subtract).then_inc(misc_free, 1)

            def invert_den(b):
                dve.wait_ge(den_in, DMA * (b + 1))
                after(dve, rden_out, DMA * b)
                nc.vector.reciprocal(rden[:], den[:]).then_inc(rden_made, 1)

            def normalise(b):
                dve.wait_ge(num_in, DMA * (b + 1))
                dve.wait_ge(rden_in, DMA * (b + 1))
                nc.vector.tensor_tensor(onorm[:], num[:], rden_all[:], ALU.mult).then_inc(norm_made, 1)

            dve.wait_ge(misc_done, 1)
            nc.vector.tensor_copy(bqk[:], misc[:, 0:2]).then_inc(misc_free, 1)
            dve.wait_ge(misc_free, 1)
            scale_and_rotate(1, 0, 0)
            scale_and_rotate(2, 0, 1)
            middle_part(0, 0)
            save_v(3, 0, 0)
            middle_part(0, 1)
            for g in range(2):
                for i in range(4):
                    for j in range(4):
                        maximum(0, g, i, j)
                if g == 0:
                    low_part(4, 0, 0)

            steps = [0]

            def chain(ins):
                steps[0] += 1
                ins.then_inc(route_step, 1)
                dve.wait_ge(route_step, steps[0])

            dve.wait_ge(lg_in, DMA)
            for t in range(2):
                chain(nc.vector.tensor_reduce(rmax[:, t:t + 1], probs[:, t, :], AX_X, ALU.max))
                chain(nc.vector.tensor_scalar(rmax[:, t:t + 1], rmax[:, t:t + 1], -1.0, None, ALU.mult))
            for t in range(2):
                dve.wait_ge(exp_made, t + 1)
                chain(nc.vector.reciprocal(rz[:, t:t + 1], zsum[:, t:t + 1]))
                chain(nc.vector.tensor_scalar(probs[:, t, :], probs[:, t, :], rz[:, t:t + 1], None, ALU.mult))
                for r in range(CAP // 8):
                    top = vals[:, t, 8 * r:8 * r + 8]
                    chain(nc.vector.max(top, probs[:, t, :]))
                    chain(nc.vector.max_index(idx[:, t, 8 * r:8 * r + 8], top, probs[:, t, :]))
                    if r < CAP // 8 - 1:
                        chain(nc.vector.match_replace(probs[:, t, :], top, probs[:, t, :], -1.0))
                chain(nc.vector.tensor_reduce(zsum[:, t:t + 1], vals[:, t, :], AX_X, ALU.add))
                chain(nc.vector.tensor_scalar(zsum[:, t:t + 1], zsum[:, t:t + 1], W_EPS, None, ALU.add))
                chain(nc.vector.reciprocal(zsum[:, t:t + 1], zsum[:, t:t + 1]))
                chain(nc.vector.tensor_scalar(route_in[:, 2 + t, :], vals[:, t, :], zsum[:, t:t + 1], None, ALU.mult))
                chain(nc.vector.tensor_scalar(route_in[:, t, :], idx[:, t, :], row_base[:, t:t + 1], None, ALU.add))
            assert steps[0] == ROUTE_STEPS
            dve.wait_ge(misc_done, 6)
            for bl in range(4):
                for n, dst in ((0, idx_all), (1, w_all)):
                    src = misc[0:CAP, 2 * n * P:2 * (n + 1) * P].rearrange("c (t r e) -> c e t r", t=4, r=4)[:, :, :, bl]
                    last = nc.vector.tensor_copy(dst[32 * bl:32 * bl + 32, :].rearrange("c (e t) -> c e t", e=E), src)
            last.then_inc(misc_free, 1)

            def body(bt):
                b, par = bt.n, bt.par
                for s in range(16):
                    g, i = divmod(s, 4)
                    for j in range(4):
                        if g < 2:
                            maximum(b, g + 2, i, j)
                        elif not bt.last:
                            maximum(b + 1, g - 2, i, j)
                        if j == 1:
                            task(bt, s - 1)
                        if j == 3 and s == 3 and not bt.first:
                            invert_den(b - 1)
                        if j == 3 and s == 8 and not bt.first:
                            after(dve, misc_done, task_no(bt, "c0"))
                            normalise(b - 1)

            def task(bt, s):
                b, par, g = bt.n, bt.par, s // 4
                name = TASK_AT.get(s)
                if name not in tasks(bt):
                    return
                no = task_no(bt, name)
                if name[0] == "c":
                    low_part(no, 4 * b + g + 1, (g + 1) % 2)
                elif name == "q":
                    scale_and_rotate(no, b + 1, 0)
                elif name == "k":
                    scale_and_rotate(no, b + 1, 1)
                    middle_part(b + 1, 0)
                elif name == "v":
                    save_v(no, b + 1, 1 - par)
                    middle_part(b + 1, 1)
                elif name[0] == "g":
                    dve.wait_ge(th_made, 2 * b + int(name[-1]) + 1)
                    nc.vector.scalar_tensor_tensor(gated[:], th[:], 1.0, misc, ALU.add, ALU.mult
                                                   ).then_inc(misc_free, 1)
                elif name[:-1] == "value":
                    dve.wait_ge(misc_done, no + 1)
                    nc.vector.scalar_tensor_tensor(hT[:, int(name[-1]), :], misc, 0.5, gated[:], ALU.mult,
                                                   ALU.mult).then_inc(misc_free, 1)
                elif name == "y":
                    dve.wait_ge(misc_done, no + 1)
                    after(dve, added, DMA * 5 * b)
                    nc.vector.tensor_tensor(
                        ys[:], misc.rearrange("p (t d) -> p t d", t=T),
                        w_all[:, bass.ds(b * T, T)].rearrange("p (t a) -> p t a", a=1).broadcast_to([P, T, D]),
                        ALU.mult).then_inc(misc_free, 1)

            batches(dve, body)
            invert_den(B - 1)
            normalise(B - 1)

        @block.gpsimd
        def _(pool):
            def pool_after(semaphore, count, nth):
                after(pool, semaphore, count)
                after(pool, paced, nth)
                nc.gpsimd.tensor_tensor(pace[:], minus_half[:, 0:1], minus_half[:, 0:1], ALU.add
                                        ).then_inc(paced, 1)

            nc.gpsimd.memset(minus_half[:], -0.5).then_inc(half_set, 1)
            pool.wait_ge(half_set, 1)

            pool.wait_ge(consts_in, DMA * N_CONSTS)

            def route_body(b, par, first):
                after(pool, var_made, b + 1)
                nc.gpsimd.tensor_tensor(rstd[:], var_eps[:], minus_half[:], ALU.pow).then_inc(rstd_made, 1)
                after(pool, xn_made, b + 1)
                after(pool, xb_out[par], before(b, par))
                nc.gpsimd.tensor_tensor(xb[:, par], xt[:, par], bout_all[:].rearrange("p (a d) -> p a d", a=1)
                                        .broadcast_to([P, T, D]), ALU.add).then_inc(xb_made, 1)
                after(pool, xb_made, b + 1)
                pool.dma_start(out_rows[bass.ds(b * S, S), :].rearrange("(t p) d -> p t d", p=P), xb[:, par]
                               ).then_inc(xb_out[par], DMA)

            phase1(pool, route_body)

            def subtract(b, n, part):
                after(pool, cast_done, 4 * b + 2 * (part - 1) + n + 1)
                if part == 1:
                    nc.gpsimd.tensor_tensor(rest[:, n], full[:, n], split[:, n, 0, :], ALU.subtract
                                            ).then_inc(sub_done, 1)
                else:
                    nc.gpsimd.tensor_tensor(split[:, n, 2, :], rest[:, n], split[:, n, 1, :], ALU.subtract
                                            ).then_inc(sub_done, 1)

            def four_subtractions(b):
                for part in (1, 2):
                    for n in range(2):
                        subtract(b, n, part)

            def gather(b, par, nth):
                nc.gpsimd.tensor_copy(idx_now[:, par], idx_all[:, bass.ds(b * T, T)]).then_inc(idx_copied, 1)
                pool_after(idx_copied, b + 1, nth)
                for t in range(T):
                    nc.gpsimd.indirect_dma_start(xg[:, par, t, :], None, xn_rows, bass.IndirectOffsetOnAxis(
                        ap=idx_now[:, par, t:t + 1], axis=0)).then_inc(gathered[par], DMA)

            def add_expert(b, par, nth):
                for t in range(T):
                    nc.gpsimd.indirect_dma_start(out_rows, bass.IndirectOffsetOnAxis(
                        ap=idx_now[:, par, t:t + 1], axis=0), ys[:, t, :], None, compute_op=ALU.add
                    ).then_inc(added, DMA)
                    pool_after(added, DMA * 5 * b + DMA * (t + 1), nth + t)

            def add_attention(b, nth):
                pool.dma_start(out_rows[bass.ds(b * S, S), :].rearrange("(t p) d -> p t d", p=P), att[:],
                               accum_op=ALU.add).then_inc(added, DMA)
                pool_after(added, DMA * 5 * b + DMA * 5, nth)

            four_subtractions(0)
            pool_after(misc_free, 6, 0)
            for par in range(2):
                pool_after(xn_out[par], DMA * B // 2, 2 * par + 1)
                pool_after(xb_out[par], DMA * B // 2, 2 * par + 2)
            gather(0, 0, 5)

            def body(bt):
                b, par = bt.n, bt.par
                nth = 7 + 9 * (b - 1)
                if not bt.last:
                    four_subtractions(b + 1)
                if bt.first:
                    gather(1, 1, 6)
                    return
                pool_after(misc_free, task_no(bt, "c0"), nth)
                add_expert(b - 1, 1 - par, nth + 1)
                pool_after(misc_free, task_no(bt, "o") + 1, nth + 5)
                add_attention(b - 1, nth + 6)
                if not bt.last:
                    pool_after(misc_done, task_no(bt, "c0"), nth + 7)
                    gather(b + 1, 1 - par, nth + 8)

            batches(pool, body)
            end = task_no(Batch(B - 1, 1, False, True), "y") + 1
            nth = 7 + 9 * (B - 1) - 2
            pool_after(misc_free, end, nth)
            add_expert(B - 1, 1, nth + 1)
            pool_after(misc_free, end + 1, nth + 5)
            add_attention(B - 1, nth + 6)


ROUTE_STEPS = 4 + 2 * (2 + 3 * (CAP // 8) - 1 + 5)


def v_task_of_prev(bt):
    order = [n for n in TASK_AT.values()]
    if isinstance(bt.n, int) and bt.n == 1:
        return len(PROLOGUE) + order.index("v")
    return len(PROLOGUE) + len(TASK_AT) * (bt.n - 1) - 1 + order.index("v")


_INS = ['L0_attn_x', 'L0_attn_Wqkv', 'L0_attn_bqkv', 'L0_attn_Wout', 'L0_attn_bout', 'L0_ffn_router_w1',
        'L0_ffn_router_w2', 'L0_ffn_w1', 'L0_ffn_w2', 'L0_ffn_w3']


def kernel(**inputs):
    import numpy as _np
    import concourse.bacc as _bacc
    import ml_dtypes
    from concourse import mybir as _mybir
    from concourse.bass_utils import run_bass_kernel_spmd as _run

    nc = _bacc.Bacc("TRN2", target_bir_lowering=False, num_devices=1)
    arrays, args = {}, []
    for name in _INS:
        a = _np.ascontiguousarray(inputs[name])
        arrays[f"in_{name}_dram"] = a
        args.append(nc.dram_tensor(f"in_{name}_dram", a.shape, _mybir.dt.from_np(a.dtype), kind="ExternalInput").ap())
    shape = inputs['L0_attn_x'].shape
    arrays["table_dram"] = constants(shape[1])
    args.append(nc.dram_tensor("table_dram", arrays["table_dram"].shape, F32, kind="ExternalInput").ap())
    arrays["fill_dram"] = _np.repeat(_np.array([[0], [1], [1]], dtype=ml_dtypes.bfloat16), HEADS * shape[1], axis=1)
    args.append(nc.dram_tensor("fill_dram", arrays["fill_dram"].shape, BF16, kind="ExternalInput").ap())
    args.append(nc.dram_tensor("out_dram", shape, F32, kind="ExternalOutput").ap())
    attention_and_experts(nc, *args)
    r = _run(nc, [arrays], core_ids=[0])
    return r.results[0]["out_dram"]
```

```python
from collections import namedtuple
from contextlib import ExitStack

import numpy as np

import concourse.bass as bass
from concourse import mybir

F32 = mybir.dt.float32
BF16 = mybir.dt.bfloat16
I32 = mybir.dt.int32
U32 = mybir.dt.uint32
ALU = mybir.AluOpType
ACT = mybir.ActivationFunctionType
AX_X = mybir.AxisListType.X

P = 128
HEADS = 16
HD = 8
CAP = 32
LN_EPS = 1e-5
W_EPS = 1e-9
DMA = 16

G = 4
KB = 4
Q_PARTS = (0, 1, 2, 0, 1, 0)
K_PARTS = (0, 0, 0, 1, 1, 2)
SCORE_ROWS = 96
STACK_ROWS = 98

TASK_AT = {0: "c0", 1: "q", 2: "k", 3: "v", 4: "c1", 5: "xe", 6: "gate0", 7: "value0", 8: "c2", 9: "o",
           10: "gate1", 11: "value1", 12: "c3", 13: "y"}
PROLOGUE = ["bias", "q", "k", "v", "c", "route"]
Batch = namedtuple("Batch", "n par first last")


def constants(S):
    theta = (10000.0 ** (-np.arange(0, HD, 2, dtype=np.float32) / HD)).astype(np.float32)
    freqs = np.arange(S, dtype=np.float32)[:, None] * theta[None, :]
    emb = np.concatenate([np.sin(freqs), np.cos(freqs)], axis=-1).astype(np.float32)
    table = np.zeros((P, S + P + 2), np.float32)
    table[:, :S] = np.repeat(emb.T, HEADS, axis=0)
    table[:, S:S + P] = np.eye(P, dtype=np.float32)
    for t in range(2):
        table[:, S + P + t] = S * (8 * t + np.arange(P) // 16)
    return table


def attention_and_experts(nc, x, Wqkv, bqkv, Wout, bout, rw1, rw2, w1, w2, w3, table, fill, out):
    B, S, D = x.shape
    E, _, FF = w1.shape
    T = S // P
    NF = FF // P
    assert (D, S, T, E, B, NF) == (P, 512, KB, 16, 16, 2)
    SCALE = float(HD) ** -0.5

    rows = x.rearrange("b s d -> (b s) d")
    out_rows = out.rearrange("b s d -> (b s) d")
    xn_rows = nc.dram_tensor("xn_rows", (B * S, D), F32).ap()
    xT_dram = nc.dram_tensor("xT_dram", (B * P, S), F32).ap()
    logits_dram = nc.dram_tensor("logits_dram", (B * E, S), F32).ap()
    split_dram = nc.dram_tensor("split_dram", (2, 2, 3, P, S), BF16).ap()
    o_dram = nc.dram_tensor("o_dram", (2, HEADS, HD + 1, S), F32).ap()
    rden_dram = nc.dram_tensor("rden_dram", (2, HEADS, S), F32).ap()

    with ExitStack() as ctx:
        def sb(name, shape, dt=F32):
            return ctx.enter_context(nc.sbuf_tensor(name, shape, dt))

        def sem(name):
            return ctx.enter_context(nc.semaphore(name))

        consts = sb("consts", [P, S + P + 2])
        emb = consts[:, 0:S]
        ident = consts[:, S:S + P]
        row_base = consts[:, S + P:S + P + 2]
        wqkv = sb("wqkv", [P, 3 * D])
        wqk = sb("wqk", [P, 2, D])
        wo = sb("wo", [P, D])
        rw1_sb = sb("rw1_sb", [P, P])
        rw2_sb = sb("rw2_sb", [P, E])
        bias_row = sb("bias_row", [1, 3 * D])
        bqk_row = sb("bqk_row", [1, 2, D])
        one = sb("one", [1, 1])
        bqk = sb("bqk", [P, 2])
        bv_all = sb("bv_all", [P, D])
        bout_all = sb("bout_all", [P, D])

        xb = sb("xb", [P, 2, T, D])
        xT = sb("xT", [P, 4, S])
        stats = sb("stats", [P, 2, T, 6])
        mean = sb("mean", [P, 2, T])
        apart = sb("apart", [P, 2, T])
        var_in = sb("var_in", [P, 2, T])
        pace = sb("pace", [P, 1])
        var_eps = sb("var_eps", [P, 2, T])
        minus_half = sb("minus_half", [P, T])
        rstd = sb("rstd", [P, 2, T])
        rt = sb("rt", [P, 2, S])
        rh = sb("rh", [P, 2, S])
        lg = sb("lg", [E, 2, S])

        router = sb("router", [P, 2, S])
        etop = sb("etop", [P, 2, CAP])
        rmax = sb("rmax", [P, 2])
        zsum = sb("zsum", [P, 2])
        tsum = sb("tsum", [P, 2])
        vals = sb("vals", [P, 2, CAP])
        idx = sb("idx", [P, 2, CAP], U32)
        route_in = sb("route_in", [P, 4, CAP])
        idx_all = sb("idx_all", [P, E * T], I32)
        w_all = sb("w_all", [P, E * T])
        idx_now = sb("idx_now", [P, 2, T], I32)

        q_stack = sb("q_stack", [P, 2, HEADS, S], BF16)
        k_stack = sb("k_stack", [P, 2, HEADS, S], BF16)
        full = sb("full", [P, 2, S])
        rest = sb("rest", [P, 2, S])
        split = sb("split", [P, 2, 3, S], BF16)
        v_ones = sb("v_ones", [P, 2, KB, HEADS, 32])
        mx = sb("mx", [P, 2, 16])
        cmax = sb("cmax", [16, 2, 2, P], BF16)
        probsT = sb("probsT", [P, 8, S])
        xt = probsT[:, 0:4, :].rearrange("p a (t d) -> p a t d", t=T)
        xn = probsT[:, 4:8, :].rearrange("p a (t d) -> p a t d", t=T)
        oT = sb("oT", [P, 2, S])
        num = sb("num", [P, S])
        den = sb("den", [P, S // 8])
        rden = sb("rden", [P, S // 8])
        rden_all = sb("rden_all", [P, S])
        onorm = sb("onorm", [P, S])
        att = sb("att", [P, T, D])

        w12 = sb("w12", [P, 2, 2, FF])
        w3_sb = sb("w3_sb", [P, 2, NF, D])
        xg = sb("xg", [P, 2, T, D])
        xe = sb("xe", [P, S])
        th = sb("th", [P, S])
        gated = sb("gated", [P, S])
        hT = sb("hT", [P, NF, S])
        ys = sb("ys", [P, T, D])

        psum = ctx.enter_context(nc.psum_tensor("psum", [P, 8, 512], F32))
        SM, ST, PV, MISC = (0, 1, 2), (3, 4, 5), 6, 7
        misc = psum[:, MISC, :]

        consts_in = sem("consts_in")
        weights_in = sem("weights_in")
        wo_in = sem("wo_in")
        ones_set = sem("ones_set")
        v_ones_set = sem("v_ones_set")
        half_set = sem("half_set")
        paced = sem("paced")
        fill_in = [sem("fill_in0"), sem("fill_in1")]
        wqk_made = sem("wqk_made")
        x_in = [sem(f"x_in{n}") for n in range(4)]
        ln_step = sem("ln_step")
        var_made = sem("var_made")
        rstd_made = sem("rstd_made")
        xn_made = sem("xn_made")
        xb_made = sem("xb_made")
        xT_done = sem("xT_done")
        xT_kept = sem("xT_kept")
        xT_made = sem("xT_made")
        hid_done = sem("hid_done")
        rt_made = sem("rt_made")
        rh_made = sem("rh_made")
        lg_done = sem("lg_done")
        lg_made = sem("lg_made")
        xn_out = [sem(f"xn_out{n}") for n in range(4)]
        xT_out = [sem(f"xT_out{n}") for n in range(4)]
        lg_out = [sem("lg_out0"), sem("lg_out1")]
        xb_out = [sem("xb_out0"), sem("xb_out1")]

        lg_in = [sem("lg_in0"), sem("lg_in1")]
        route_step = sem("route_step")
        exp_made = sem("exp_made")
        idx_copied = sem("idx_copied")

        xT_in = [sem("xT_in0"), sem("xT_in1")]
        w_in = [sem("w_in0"), sem("w_in1")]
        high_done = sem("high_done")
        middle_done = sem("middle_done")
        sub_done = sem("sub_done")
        split_out = sem("split_out")
        stacks_in = sem("stacks_in")
        sm_done = sem("sm_done")
        max_done = sem("max_done")
        chi_made = sem("chi_made")
        cmax_in = sem("cmax_in")
        st_done = sem("st_done")
        exp_done = sem("exp_done")
        pv_done = sem("pv_done")
        oT_made = sem("oT_made")
        oT_out = [sem("oT_out0"), sem("oT_out1")]
        num_in = sem("num_in")
        den_in = sem("den_in")
        rden_made = sem("rden_made")
        rden_out = sem("rden_out")
        rden_in = sem("rden_in")
        norm_made = sem("norm_made")
        misc_done = sem("misc_done")
        misc_free = sem("misc_free")
        th_made = sem("th_made")
        gathered = [sem("gathered0"), sem("gathered1")]
        added = sem("added")

        def after(eng, semaphore, count):
            if not (isinstance(count, int) and count <= 0):
                eng.wait_ge(semaphore, count)

        def through(b, par, per=DMA):
            return (b - par) * (per // 2) + per

        def before(b, par, per=DMA):
            return (b - par) * (per // 2)

        def ring(g, i, j):
            k = 16 * g + 4 * i + j
            return (k % 3 if k < 62 else (0, 2)[k - 62]), {62: 2, 63: 4, 0: 2, 1: 4}.get(k, 3)

        def among_first(b, number):
            return isinstance(b, int) and b < number

        def is_row(b, number):
            return isinstance(b, int) and b == number

        def after_all(eng, semaphores, count):
            for semaphore in semaphores:
                eng.wait_ge(semaphore, count)

        def tasks(bt):
            names = list(TASK_AT.values())
            if bt.first:
                names.remove("o")
            if bt.last:
                names = [n for n in names if n not in ("q", "k", "v", "c3")]
            return names

        def task_no(bt, name):
            if bt is None:
                return PROLOGUE.index(name)
            start = len(PROLOGUE) if bt.first else len(PROLOGUE) + len(TASK_AT) * bt.n - 1
            return start + tasks(bt).index(name)

        def batches(eng, body):
            body(Batch(0, 0, True, False))
            body(Batch(1, 1, False, False))
            with eng.Fori(1, B // 2 - 1) as i:
                body(Batch(2 * i, 0, False, False))
                body(Batch(2 * i + 1, 1, False, False))
            body(Batch(B - 2, 0, False, False))
            body(Batch(B - 1, 1, False, True))

        def phase1(body, b=None):
            for u in range(4):
                body(u if b is None else b + u, u % 2, u)

        def ahead(b, u):
            return b * (DMA // 4) + (DMA - u * (DMA // 4))

        block = ctx.enter_context(nc.Block())
        N_CONSTS, N_WEIGHTS = 4, 3

        @block.sync
        def _(sp):
            def load_x(b, u):
                after(sp, xn_made, b - 3)
                after(sp, xb_made, b - 3)
                sp.dma_start(xt[:, u], rows[bass.ds(b * S, S), :].rearrange("(t p) d -> p t d", p=P)
                             ).then_inc(x_in[u], DMA)

            def store_row(b, par, u):
                after(sp, xn_made, b + 1)
                sp.dma_start(xn_rows[bass.ds(b * S, S), :].rearrange("(t p) d -> p t d", p=P), xn[:, u]
                             ).then_inc(xn_out[u], DMA)
                after(sp, xb_made, b + 1)
                sp.dma_start(out_rows[bass.ds(b * S, S), :].rearrange("(t p) d -> p t d", p=P), xb[:, par]
                             ).then_inc(xb_out[par], DMA)
                after(sp, xT_made, b + 1)
                sp.dma_start(xT_dram[bass.ds(b * P, P), :], xT[:, u]).then_inc(xT_out[u], DMA)

            load_x(0, 0)
            sp.dma_start(consts[:], table).then_inc(consts_in, DMA)
            sp.dma_start(rw1_sb[:], rw1).then_inc(consts_in, DMA)
            sp.dma_start(rw2_sb[:], rw2).then_inc(consts_in, DMA)
            sp.dma_start(bout_all[:], bout.rearrange("(a d) -> a d", a=1).broadcast_to([P, D])).then_inc(consts_in, DMA)
            load_x(1, 1)
            sp.dma_start(wqkv[:], Wqkv).then_inc(weights_in, DMA)
            sp.dma_start(bias_row[:], bqkv.rearrange("(a d) -> a d", a=1)).then_inc(weights_in, DMA)
            sp.dma_start(bv_all[:], bqkv[2 * D:3 * D].rearrange("(a d) -> a d", a=1).broadcast_to([P, D])
                         ).then_inc(weights_in, DMA)
            load_x(2, 2)
            load_x(3, 3)
            sp.dma_start(wo[:], Wout.rearrange("(h d) n -> d h n", d=HD)).then_inc(wo_in, DMA)

            def store_parts(b, par):
                after(sp, stacks_in, 6 * DMA * (b - 1))
                after(sp, sub_done, 4 * b + 3)
                sp.dma_start(split_dram[par, 0].rearrange("q p s -> p q s"), split[:, 0]).then_inc(split_out, DMA)
                after(sp, sub_done, 4 * b + 4)
                sp.dma_start(split_dram[par, 1].rearrange("q p s -> p q s"), split[:, 1]).then_inc(split_out, DMA)

            def fill_stacks(b, par):
                after(sp, split_out, 2 * DMA * b + 2 * DMA)
                at = 0
                for part, n in enumerate((3, 2, 1)):
                    sp.dma_start(q_stack[at:at + 8 * n, par], split_dram[par, 0, 0:n].rearrange(
                        "q (d h) s -> (q d) h s", h=HEADS)).then_inc(stacks_in, DMA)
                    sp.dma_start(k_stack[at:at + 8 * n, par], split_dram[par, 1, part:part + 1].rearrange(
                        "q (d h) s -> q d h s", h=HEADS).broadcast_to([n, HD, HEADS, S])).then_inc(stacks_in, DMA)
                    at += 8 * n

            def first_rows(b, par, u):
                store_row(b, par, u)
                load_x(b + 4, u)

            def clear_unused_rows(par):
                unused = SCORE_ROWS - 8 * len(Q_PARTS)
                for stack in (q_stack, k_stack):
                    sp.dma_start(stack[SCORE_ROWS - unused:SCORE_ROWS, par].rearrange("p h s -> p (h s)"),
                                 fill[0:1, :].broadcast_to([unused, HEADS * S])).then_inc(fill_in[par], DMA)
                sp.dma_start(k_stack[SCORE_ROWS:STACK_ROWS, par].rearrange("p h s -> p (h s)"),
                             fill[1:2, :].broadcast_to([2, HEADS * S])).then_inc(fill_in[par], DMA)

            clear_unused_rows(0)
            with sp.Fori(0, 2) as i:
                phase1(first_rows, 4 * i)
            store_parts(0, 0)
            phase1(first_rows, 8)

            def load_logits(t):
                after_all(sp, lg_out, DMA * (t + 1) * B // 4)
                sp.dma_start(router[:, t], logits_dram.rearrange("(t p) s -> t p s", p=P)[t]).then_inc(lg_in[t], DMA)

            def last_rows(b, par, u):
                store_row(b, par, u)
                if u == 0:
                    load_logits(0)
                elif u == 1:
                    fill_stacks(0, 0)

            phase1(last_rows, B - 4)
            for n, w in enumerate((w1, w2)):
                sp.dma_start(w12[:, 0, n, :], w[0]).then_inc(w_in[0], DMA)
            sp.dma_start(w3_sb[:, 0], w3[0].rearrange("(f p) d -> p f d", p=P)).then_inc(w_in[0], DMA)

            clear_unused_rows(1)
            load_logits(1)

            def load_xT(b, par):
                after_all(sp, xT_out, DMA * B // 4)
                sp.dma_start(xT[:, par], xT_dram[bass.ds(b * P, P), :]).then_inc(xT_in[par], DMA)

            after(sp, hid_done, B)
            load_xT(1, 1)

            def move_cmax(v, par, gg, task):
                cp = gg % 2
                after(sp, misc_free, task + 1)
                after(sp, st_done, 16 * (v - 7))
                for r in range(2):
                    sp.dma_start(q_stack[SCORE_ROWS + r:SCORE_ROWS + r + 1, par, G * gg:G * gg + G, :].rearrange(
                        "r h (b q) -> r (h b) q", b=KB), cmax[:, cp, r, :]).then_inc(cmax_in, DMA)

            def store_oT(b, par, g):
                after(sp, oT_made, 4 * b + g + 1)
                for j in range(G):
                    sp.dma_start(o_dram[par, G * g + j], oT[32 * j:32 * j + HD + 1, g % 2, :]
                                 ).then_inc(oT_out[g % 2], DMA)

            def load_den(b, par):
                after_all(sp, oT_out, 2 * G * DMA * (b + 1))
                after(sp, rden_made, b)
                sp.dma_start(den[:], o_dram[par, :, HD].rearrange("h (c s) -> h c s", c=8)).then_inc(den_in, DMA)
                after(sp, norm_made, b)
                sp.dma_start(num[:], o_dram[par, :, 0:HD].rearrange("h d s -> d h s")).then_inc(num_in, DMA)

            def store_rden(b, par):
                after(sp, rden_made, b + 1)
                sp.dma_start(rden_dram[par].rearrange("h (c s) -> (h c) s", c=8), rden[:]).then_inc(rden_out, DMA)

            def spread_rden(b, par):
                after(sp, rden_out, DMA * (b + 1))
                sp.dma_start(rden_all[:], rden_dram[par:par + 1].broadcast_to([HD, HEADS, S])).then_inc(rden_in, DMA)

            move_cmax(0, 0, 0, task_no(None, "c"))

            def body(bt):
                b, par = bt.n, bt.par
                if not bt.last:
                    if not bt.first:
                        prev = task_no(Batch(b, par, False, False), "c0") - 1
                        after(sp, misc_done, prev + 1)
                    for n, w in enumerate((w1, w2)):
                        sp.dma_start(w12[:, 1 - par, n, :], w.rearrange("e p f -> (e p) f")[bass.ds((b + 1) * P, P), :]
                                     ).then_inc(w_in[1 - par], DMA)
                    sp.dma_start(w3_sb[:, 1 - par], w3.rearrange("e f d -> (e f) d")[bass.ds((b + 1) * FF, FF), :]
                                 .rearrange("(f p) d -> p f d", p=P)).then_inc(w_in[1 - par], DMA)
                move_cmax(4 * b + 1, par, 1, task_no(bt, "c0"))
                if not bt.first:
                    store_oT(b - 1, 1 - par, 3)
                    load_den(b - 1, 1 - par)
                if not bt.last:
                    store_parts(b + 1, 1 - par)
                if not bt.first:
                    store_rden(b - 1, 1 - par)
                move_cmax(4 * b + 2, par, 2, task_no(bt, "c1"))
                if not bt.last:
                    fill_stacks(b + 1, 1 - par)
                    if not is_row(b, B - 2):
                        after(sp, misc_done, task_no(bt, "c0"))
                        load_xT(b + 2, par)
                if not bt.first:
                    spread_rden(b - 1, 1 - par)
                store_oT(b, par, 0)
                move_cmax(4 * b + 3, par, 3, task_no(bt, "c2"))
                store_oT(b, par, 1)
                if not bt.last:
                    move_cmax(4 * b + 4, 1 - par, 0, task_no(bt, "c3"))
                store_oT(b, par, 2)

            batches(sp, body)
            store_oT(B - 1, 1, 3)
            load_den(B - 1, 1)
            store_rden(B - 1, 1)
            spread_rden(B - 1, 1)

        @block.tensor
        def _(pe):
            pe.wait_ge(consts_in, DMA * N_CONSTS)

            def logits(b, par):
                pe.wait_ge(rh_made, b + 1)
                after(pe, lg_made, b - 1)
                nc.tensor.matmul(psum[0:E, 4 + par, :], rw2_sb[:], rh[:, par], start=True, stop=True
                                 ).then_inc(lg_done, 1)

            def route_body(b, par, u):
                pe.wait_ge(xn_made, b + 1)
                after(pe, xT_made, b - 1)
                for t in range(T):
                    last = nc.tensor.transpose(psum[:, par, t * P:(t + 1) * P], xn[:, u, t, :], ident)
                last.then_inc(xT_done, 1)
                if not among_first(b, 2):
                    logits(b - 2, par)
                pe.wait_ge(xT_made, b + 1)
                after(pe, rh_made, b - 1)
                nc.tensor.matmul(psum[:, 2 + par, :], rw1_sb[:], xT[:, u], start=True, stop=True
                                 ).then_inc(hid_done, 1)

            def start_task(no):
                after(pe, misc_free, no)

            def xT_of(b, par):
                return xe[:] if is_row(b, 0) else xT[:, par]

            def project_qk(no, b, par, n):
                if n == 0 and not is_row(b, 0):
                    pe.wait_ge(xT_in[par], before(b, par) if par == 0 else through(b, par))
                start_task(no)
                nc.tensor.matmul(misc, wqk[:, n, :], xT_of(b, par), start=True, stop=True).then_inc(misc_done, 1)

            def project_v(no, b, par):
                start_task(no)
                for t in range(T):
                    last = nc.tensor.matmul(misc[:, t * P:(t + 1) * P], xT_of(b, par)[:, t * P:(t + 1) * P],
                                            wqkv[:, 2 * D:3 * D], start=True, stop=True)
                last.then_inc(misc_done, 1)

            def transpose_max(no, v, gp):
                pe.wait_ge(max_done, 16 * v + 16)
                start_task(no)
                nc.tensor.transpose(misc[0:16, 0:P], mx[:, gp, :], ident).then_inc(misc_done, 1)

            def score_for_max(b, par, g, i, j):
                n = 64 * b + 16 * g + 4 * i + j
                if (g, i, j) == (0, 0, 0):
                    pe.wait_ge(stacks_in, 6 * DMA * b + 6 * DMA)
                    if is_row(b, 1):
                        pe.wait_ge(fill_in[1], 3 * DMA)
                bank, ago = ring(g, i, j)
                after(pe, max_done, n - ago + 1)
                h = G * g + i
                nc.tensor.matmul(psum[:, SM[bank], :], q_stack[0:SCORE_ROWS, par, h, j * P:(j + 1) * P],
                                 k_stack[0:SCORE_ROWS, par, h, :], start=True, stop=True).then_inc(sm_done, 1)

            def score_for_exp(b, par, g, i, j):
                m = 64 * b + 16 * g + 4 * i + j
                if (i, j) == (0, 0):
                    pe.wait_ge(cmax_in, 2 * DMA * (4 * b + g) + 2 * DMA)
                bank, ago = ring(g, i, j)
                after(pe, exp_done, m - ago + 1)
                h = G * g + j
                nc.tensor.matmul(psum[:, ST[bank], :], k_stack[0:STACK_ROWS, par, h, i * P:(i + 1) * P],
                                 q_stack[0:STACK_ROWS, par, h, :], start=True, stop=True).then_inc(st_done, 1)

            def times_v(b, par, g, i, v_task):
                step = 16 * b + 4 * g + i
                pe.wait_ge(exp_done, 4 * step + 4)
                if (g, i) == (0, 0):
                    pe.wait_ge(misc_free, v_task + 1)
                if i == 0:
                    after(pe, oT_made, 4 * b + g)
                for j in range(G):
                    last = nc.tensor.matmul(psum[32 * j:32 * j + 32, PV, :], v_ones[:, par, i, G * g + j, :],
                                            probsT[:, 4 * (i % 2) + j, :], start=(i == 0), stop=(i == KB - 1))
                last.then_inc(pv_done, 1)

            def project_out(no, b):
                pe.wait_ge(norm_made, b + 1)
                start_task(no)
                for t in range(T):
                    last = nc.tensor.matmul(misc[:, t * P:(t + 1) * P], onorm[:, t * P:(t + 1) * P], wo[:],
                                            start=True, stop=True)
                last.then_inc(misc_done, 1)

            def first_rows(b, par, u):
                route_body(b, par, u)
                if b == 0:
                    pe.wait_ge(weights_in, DMA * N_WEIGHTS)
                    pe.wait_ge(wqk_made, 2)
                    for n in range(2):
                        last = nc.tensor.matmul(misc[:, n:n + 1], bqk_row[0:1, n, :], one[0:1, 0:1], start=True,
                                                stop=True)
                    last.then_inc(misc_done, 1)
                    pe.wait_ge(xT_kept, 1)
                elif b == 1:
                    project_qk(1, 0, 0, 0)
                elif b == 2:
                    project_qk(2, 0, 0, 1)
                elif b == 3:
                    project_v(3, 0, 0)

            phase1(first_rows)
            phase1(route_body, 4)
            with pe.Fori(2, B // 4) as i:
                phase1(route_body, 4 * i)
            logits(B - 2, 0)
            logits(B - 1, 1)
            pe.wait_ge(fill_in[0], 3 * DMA)
            for g in range(2):
                for i in range(4):
                    for j in range(4):
                        score_for_max(0, 0, g, i, j)
                if g == 0:
                    transpose_max(4, 0, 0)
            pe.wait_ge(route_step, ROUTE_STEPS)
            start_task(5)
            for n in range(4):
                last = nc.tensor.transpose(misc[0:CAP, n * P:(n + 1) * P], route_in[:, n, :], ident)
            last.then_inc(misc_done, 1)

            def body(bt):
                b, par = bt.n, bt.par
                for s in range(16):
                    g, i = divmod(s, 4)
                    for j in range(4):
                        if g < 2:
                            score_for_max(b, par, g + 2, i, j)
                        elif not bt.last:
                            score_for_max(b + 1, 1 - par, g - 2, i, j)
                        score_for_exp(b, par, g, i, j)
                        if j == 2 and s:
                            times_v(b, par, (s - 1) // 4, (s - 1) % 4,
                                    task_no(None, "v") if bt.first else v_task_of_prev(bt))
                        elif j == 2 and not bt.first:
                            times_v(b - 1, 1 - par, 3, 3, None)
                    name = TASK_AT.get(s)
                    if name not in tasks(bt):
                        continue
                    no = task_no(bt, name)
                    if name[0] == "c":
                        transpose_max(no, 4 * b + g + 1, (g + 1) % 2)
                    elif name in ("q", "k"):
                        project_qk(no, b + 1, 1 - par, "qk".index(name))
                    elif name == "v":
                        project_v(no, b + 1, 1 - par)
                    elif name == "o":
                        project_out(no, b - 1)
                    elif name == "xe":
                        pe.wait_ge(gathered[par], through(b, par, T * DMA))
                        start_task(no)
                        for t in range(T):
                            last = nc.tensor.transpose(misc[:, t * P:(t + 1) * P], xg[:, par, t, :], ident)
                        last.then_inc(misc_done, 1)
                    elif name[:-1] in ("gate", "value"):
                        n, f = (0 if name[0] == "g" else 1), int(name[-1])
                        if (n, f) == (0, 0):
                            pe.wait_ge(w_in[par], through(b, par, 3 * DMA))
                        start_task(no)
                        nc.tensor.matmul(misc, w12[:, par, n, f * P:(f + 1) * P], xe[:], start=True, stop=True
                                         ).then_inc(misc_done, 1)
                    elif name == "y":
                        start_task(no)
                        for t in range(T):
                            for f in range(NF):
                                last = nc.tensor.matmul(misc[:, t * P:(t + 1) * P], hT[:, f, t * P:(t + 1) * P],
                                                        w3_sb[:, par, f, :], start=(f == 0), stop=(f == NF - 1))
                        last.then_inc(misc_done, 1)

            pe.wait_ge(lg_made, B)
            pe.wait_ge(v_ones_set, 1)
            pe.wait_ge(wo_in, DMA)
            batches(pe, body)
            times_v(B - 1, 1, 3, 3, None)
            project_out(task_no(Batch(B - 1, 1, False, True), "y") + 1, B - 1)

        @block.scalar
        def _(act):
            def middle_part(b, n):
                act.wait_ge(sub_done, 4 * b + n + 1)
                nc.scalar.copy(split[:, n, 1, :], rest[:, n]).then_inc(middle_done, 1)

            def router_out(b, par):
                act.wait_ge(lg_done, b + 1)
                after(act, lg_out[par], before(b, par))
                nc.scalar.mul(lg[:, par], psum[0:E, 4 + par, :], 0.5).then_inc(lg_made, 1)

            def store_logits(b, par):
                act.wait_ge(lg_made, b + 1)
                act.dma_start(logits_dram[bass.ds(b * E, E), :], lg[:, par]).then_inc(lg_out[par], DMA)

            def route_body(b, par, u):
                if is_row(b, 5) or is_row(b, 6):
                    middle_part(0, b - 5)
                act.wait_ge(xT_done, b + 1)
                if is_row(b, 0):
                    nc.scalar.copy(xe[:], psum[:, par, :]).then_inc(xT_kept, 1)
                if not among_first(b, 4):
                    act.wait_ge(xT_out[u], ahead(b - 4, u))
                after(act, hid_done, b - 3)
                nc.scalar.copy(xT[:, u], psum[:, par, :]).then_inc(xT_made, 1)
                if not among_first(b, 3):
                    store_logits(b - 3, 1 - par)
                act.wait_ge(hid_done, b + 1)
                after(act, rh_made, b - 1)
                nc.scalar.activation(rt[:, par], psum[:, 2 + par, :], ACT.Tanh, scale=0.5).then_inc(rt_made, 1)
                if not among_first(b, 2):
                    router_out(b - 2, par)

            phase1(route_body)
            phase1(route_body, 4)
            with act.Fori(2, B // 4) as i:
                phase1(route_body, 4 * i)
            store_logits(B - 3, 1)
            router_out(B - 2, 0)
            store_logits(B - 2, 0)
            router_out(B - 1, 1)
            store_logits(B - 1, 1)

            def high_part(no, v, gp):
                act.wait_ge(misc_done, no + 1)
                after(act, cmax_in, 2 * DMA * (v - 1))
                nc.scalar.mul(cmax[:, gp, 0, :], misc[0:16, 0:P], -1.0).then_inc(chi_made, 1)

            def router_exp(t):
                act.wait_ge(route_step, TOP_STEPS * t + 2)
                nc.scalar.activation(full[:, t, :], router[:, t, :], ACT.Exp, bias=rmax[:, t:t + 1],
                                     accum_out=zsum[:, t:t + 1])
                act.wait_ge(route_step, TOP_STEPS * t + TOP_STEPS)
                nc.scalar.activation(etop[:, t, :], vals[:, t, :], ACT.Exp, bias=rmax[:, t:t + 1],
                                     accum_out=tsum[:, t:t + 1]).then_inc(exp_made, 1)

            router_exp(0)
            high_part(4, 0, 0)
            router_exp(1)

            def save_oT(b, g):
                act.wait_ge(pv_done, 16 * b + 4 * g + 4)
                after(act, oT_out[g % 2], G * DMA * (2 * b + g // 2))
                nc.scalar.copy(oT[:, g % 2], psum[:, PV, :]).then_inc(oT_made, 1)

            def body(bt):
                b, par = bt.n, bt.par
                for s in range(16):
                    g, i = divmod(s, 4)
                    for j in range(4):
                        m = 64 * b + 4 * s + j
                        act.wait_ge(st_done, m + 1)
                        if j == 0:
                            after(act, pv_done, 16 * b + s - 1)
                        nc.scalar.activation(probsT[:, 4 * (i % 2) + j, :], psum[:, ST[ring(g, i, j)[0]], :], ACT.Exp, scale=SCALE
                                             ).then_inc(exp_done, 1)
                        if j == 0:
                            task(bt, s - 1)
                        if (s, j) in ((3, 1), (4, 1)) and not bt.last:
                            middle_part(b + 1, s - 3)
                        if j == 2 and i == 0 and not (bt.first and g == 0):
                            save_oT(b if g else b - 1, (g - 1) % 4)

            def task(bt, s):
                b, g = bt.n, s // 4
                name = TASK_AT.get(s)
                if name not in tasks(bt):
                    return
                no = task_no(bt, name)
                if name[0] == "c":
                    high_part(no, 4 * b + g + 1, (g + 1) % 2)
                elif name == "xe":
                    act.wait_ge(misc_done, no + 1)
                    nc.scalar.copy(xe[:], misc).then_inc(misc_free, 1)
                elif name == "o":
                    act.wait_ge(misc_done, no + 1)
                    after(act, added, DMA * 5 * (b - 1))
                    nc.scalar.copy(att[:].rearrange("p t d -> p (t d)"), misc).then_inc(misc_free, 1)
                elif name[0] == "g":
                    act.wait_ge(misc_done, no + 1)
                    nc.scalar.activation(th[:], misc, ACT.Tanh, scale=0.5).then_inc(th_made, 1)

            after_all(act, xn_out, DMA * B // 4)
            batches(act, body)
            save_oT(B - 1, 3)
            no = task_no(Batch(B - 1, 1, False, True), "y") + 1
            act.wait_ge(misc_done, no + 1)
            act.wait_ge(added, DMA * 5 * (B - 1))
            nc.scalar.copy(att[:].rearrange("p t d -> p (t d)"), misc).then_inc(misc_free, 1)

        @block.vector
        def _(dve):
            nc.vector.memset(one[:], 1.0).then_inc(ones_set, 1)

            def hidden(b, par):
                dve.wait_ge(rt_made, b + 1)
                after(dve, lg_done, b - 1)
                nc.vector.scalar_tensor_tensor(rh[:, par], rt[:, par], 1.0, psum[:, 2 + par, :], ALU.add, ALU.mult
                                               ).then_inc(rh_made, 1)

            def statistics(b, par, u):
                dve.wait_ge(x_in[u], ahead(b, u))
                for t in range(T):
                    last = nc.vector.bn_stats(stats[:, par, t, :], xt[:, u, t, :])
                last.then_inc(ln_step, 1)
                dve.wait_ge(ln_step, 3 * b + 1)
                even, odd = stats[:, par, :, 0:3], stats[:, par, :, 3:6]
                nc.vector.tensor_tensor(mean[:, par], even[:, :, 1], odd[:, :, 1], ALU.add)
                nc.vector.tensor_tensor(apart[:, par], even[:, :, 1], odd[:, :, 1], ALU.subtract)
                nc.vector.tensor_tensor(var_eps[:, par], even[:, :, 2], odd[:, :, 2], ALU.add).then_inc(ln_step, 1)
                dve.wait_ge(ln_step, 3 * b + 2)
                nc.vector.tensor_scalar(mean[:, par], mean[:, par], 0.5, None, ALU.mult)
                nc.vector.scalar_tensor_tensor(apart[:, par], apart[:, par], 0.25, apart[:, par], ALU.mult, ALU.mult)
                nc.vector.tensor_scalar(var_in[:, par], var_eps[:, par], 1.0 / D, LN_EPS, ALU.mult, ALU.add
                                        ).then_inc(ln_step, 1)
                dve.wait_ge(ln_step, 3 * b + 3)
                nc.vector.tensor_tensor(var_eps[:, par], var_in[:, par], apart[:, par], ALU.add).then_inc(var_made, 1)

            def layer_norm(b, par, u):
                dve.wait_ge(rstd_made, b + 1)
                if not among_first(b, 4):
                    dve.wait_ge(xn_out[u], ahead(b - 4, u))
                after(dve, xT_done, b - 3)
                for t in range(T):
                    last = nc.vector.tensor_scalar(xn[:, u, t, :], xt[:, u, t, :], mean[:, par, t:t + 1],
                                                   rstd[:, par, t:t + 1], ALU.subtract, ALU.mult)
                last.then_inc(xn_made, 1)

            def fold_weights():
                dve.wait_ge(weights_in, DMA * N_WEIGHTS)
                for src, dst in ((wqkv, wqk), (bias_row, bqk_row)):
                    v = src[:, 0:2 * D].rearrange("p (n h d) -> p n h d", n=2, h=HEADS)
                    o = dst[:].rearrange("p n (d h) -> p n h d", d=HD)
                    for n in range(2):
                        nc.vector.tensor_tensor(o[:, n, :, 0:4], v[:, n, :, 0:4], v[:, n, :, 1::2], ALU.subtract)
                        last = nc.vector.tensor_tensor(o[:, n, :, 4:8], v[:, n, :, 4:8], v[:, n, :, 0::2], ALU.add)
                    last.then_inc(wqk_made, 1)

            def scale_and_rotate(no, b, n):
                dve.wait_ge(misc_done, no + 1)
                after(dve, sub_done, 4 * (b - 1) + n + 1)
                nc.vector.scalar_tensor_tensor(full[:, n], misc, bqk[:, n:n + 1], emb, ALU.add, ALU.mult
                                               ).then_inc(misc_free, 1)
                dve.wait_ge(misc_free, no + 1)
                after(dve, split_out, 2 * DMA * b)
                nc.vector.tensor_copy(split[:, n, 0, :], full[:, n]).then_inc(high_done, 1)

            def save_v(no, b, par):
                dve.wait_ge(misc_done, no + 1)
                after(dve, pv_done, 16 * (b - 1))
                nc.vector.tensor_tensor(
                    v_ones[:, par, :, :, 0:HD], misc.rearrange("p (k h d) -> p k h d", k=KB, h=HEADS),
                    bv_all[:].rearrange("p (a h d) -> p a h d", a=1, h=HEADS).broadcast_to([P, KB, HEADS, HD]),
                    ALU.add).then_inc(misc_free, 1)

            def maximum(b, g, i, j):
                n = 64 * b + 16 * g + 4 * i + j
                dve.wait_ge(sm_done, n + 1)
                nc.vector.tensor_reduce(mx[:, g % 2, 4 * i + j:4 * i + j + 1], psum[:, SM[ring(g, i, j)[0]], :], AX_X, ALU.max
                                        ).then_inc(max_done, 1)

            def low_part(no, v, gp):
                dve.wait_ge(chi_made, v + 1)
                nc.vector.scalar_tensor_tensor(cmax[:, gp, 1, :], misc[0:16, 0:P], -1.0, cmax[:, gp, 0, :],
                                               ALU.mult, ALU.subtract).then_inc(misc_free, 1)

            def invert_den(b):
                dve.wait_ge(den_in, DMA * (b + 1))
                after(dve, rden_out, DMA * b)
                nc.vector.reciprocal(rden[:], den[:]).then_inc(rden_made, 1)

            def normalise(b):
                dve.wait_ge(num_in, DMA * (b + 1))
                dve.wait_ge(rden_in, DMA * (b + 1))
                nc.vector.tensor_tensor(onorm[:], num[:], rden_all[:], ALU.mult).then_inc(norm_made, 1)

            def route_body(b, par, u):
                statistics(b, par, u)
                if not among_first(b, 3):
                    hidden(b - 3, 1 - par)
                if not is_row(b, 0):
                    layer_norm(b - 1, 1 - par, (u - 1) % 4)
                if is_row(b, 1):
                    fold_weights()
                if is_row(b, 2):
                    dve.wait_ge(misc_done, 1)
                    nc.vector.tensor_copy(bqk[:], misc[:, 0:2]).then_inc(misc_free, 1)
                elif is_row(b, 3):
                    dve.wait_ge(misc_free, 1)
                    scale_and_rotate(1, 0, 0)
                elif is_row(b, 4):
                    scale_and_rotate(2, 0, 1)
                elif is_row(b, 5):
                    save_v(3, 0, 0)

            phase1(route_body)
            phase1(route_body, 4)
            with dve.Fori(2, B // 4) as i:
                phase1(route_body, 4 * i)
            hidden(B - 3, 1)
            layer_norm(B - 1, 1, 3)

            steps = [0]

            def chain(ins):
                steps[0] += 1
                ins.then_inc(route_step, 1)
                dve.wait_ge(route_step, steps[0])

            def next_eight(t, r):
                if r == 0:
                    dve.wait_ge(lg_in[t], DMA)
                source = router if r == 0 else rest
                top = vals[:, t, 8 * r:8 * r + 8]
                chain(nc.vector.max(top, source[:, t, :]))
                if r == 0:
                    chain(nc.vector.tensor_scalar(rmax[:, t:t + 1], vals[:, t, 0:1], -1.0, None, ALU.mult))
                chain(nc.vector.max_index(idx[:, t, 8 * r:8 * r + 8], top, source[:, t, :]))
                if r < CAP // 8 - 1:
                    chain(nc.vector.match_replace(rest[:, t, :], top, source[:, t, :], -3.0e38))

            def weights(t):
                chain(nc.vector.tensor_scalar(route_in[:, t, :], idx[:, t, :], row_base[:, t:t + 1], None, ALU.add))
                dve.wait_ge(exp_made, t + 1)
                chain(nc.vector.scalar_tensor_tensor(tsum[:, t:t + 1], zsum[:, t:t + 1], W_EPS, tsum[:, t:t + 1],
                                                     ALU.mult, ALU.add))
                chain(nc.vector.reciprocal(tsum[:, t:t + 1], tsum[:, t:t + 1]))
                chain(nc.vector.tensor_scalar(route_in[:, 2 + t, :], etop[:, t, :], tsum[:, t:t + 1], None, ALU.mult))

            next_eight(0, 0)
            hidden(B - 2, 0)
            hidden(B - 1, 1)
            next_eight(0, 1)
            next_eight(0, 2)
            next_eight(0, 3)
            for g in range(2):
                for i in range(4):
                    for j in range(4):
                        maximum(0, g, i, j)
                if g == 0:
                    low_part(4, 0, 0)
            for r in range(CAP // 8):
                next_eight(1, r)
            assert steps[0] == 2 * TOP_STEPS
            weights(0)
            weights(1)
            assert steps[0] == ROUTE_STEPS
            dve.wait_ge(misc_done, 6)
            for bl in range(4):
                for n, dst in ((0, idx_all), (1, w_all)):
                    src = misc[0:CAP, 2 * n * P:2 * (n + 1) * P].rearrange("c (t r e) -> c e t r", t=4, r=4)[:, :, :, bl]
                    last = nc.vector.tensor_copy(dst[32 * bl:32 * bl + 32, :].rearrange("c (e t) -> c e t", e=E), src)
            last.then_inc(misc_free, 1)

            def body(bt):
                b, par = bt.n, bt.par
                for s in range(16):
                    g, i = divmod(s, 4)
                    for j in range(4):
                        if g < 2:
                            maximum(b, g + 2, i, j)
                        elif not bt.last:
                            maximum(b + 1, g - 2, i, j)
                        if j == 0:
                            task(bt, s - 1)
                        if j == 3 and s == 3 and not bt.first:
                            invert_den(b - 1)
                        if j == 3 and s == 8 and not bt.first:
                            after(dve, misc_done, task_no(bt, "c0"))
                            normalise(b - 1)

            def task(bt, s):
                b, par, g = bt.n, bt.par, s // 4
                name = TASK_AT.get(s)
                if name not in tasks(bt):
                    return
                no = task_no(bt, name)
                if name[0] == "c":
                    low_part(no, 4 * b + g + 1, (g + 1) % 2)
                elif name == "q":
                    scale_and_rotate(no, b + 1, 0)
                elif name == "k":
                    scale_and_rotate(no, b + 1, 1)
                elif name == "v":
                    save_v(no, b + 1, 1 - par)
                elif name[0] == "g":
                    dve.wait_ge(th_made, 2 * b + int(name[-1]) + 1)
                    nc.vector.scalar_tensor_tensor(gated[:], th[:], 1.0, misc, ALU.add, ALU.mult
                                                   ).then_inc(misc_free, 1)
                elif name[:-1] == "value":
                    dve.wait_ge(misc_done, no + 1)
                    nc.vector.scalar_tensor_tensor(hT[:, int(name[-1]), :], misc, 0.5, gated[:], ALU.mult,
                                                   ALU.mult).then_inc(misc_free, 1)
                elif name == "y":
                    dve.wait_ge(misc_done, no + 1)
                    after(dve, added, DMA * 5 * b)
                    nc.vector.tensor_tensor(
                        ys[:], misc.rearrange("p (t d) -> p t d", t=T),
                        w_all[:, bass.ds(b * T, T)].rearrange("p (t a) -> p t a", a=1).broadcast_to([P, T, D]),
                        ALU.mult).then_inc(misc_free, 1)

            batches(dve, body)
            invert_den(B - 1)
            normalise(B - 1)

        @block.gpsimd
        def _(pool):
            def pool_after(semaphore, count, nth):
                after(pool, semaphore, count)
                after(pool, paced, nth)
                nc.gpsimd.tensor_tensor(pace[:], minus_half[:, 0:1], minus_half[:, 0:1], ALU.add
                                        ).then_inc(paced, 1)

            nc.gpsimd.memset(minus_half[:], -0.5).then_inc(half_set, 1)
            pool.wait_ge(half_set, 1)

            def route_body(b, par, u):
                after(pool, var_made, b + 1)
                nc.gpsimd.tensor_tensor(rstd[:, par], var_eps[:, par], minus_half[:], ALU.pow).then_inc(rstd_made, 1)
                if is_row(b, 0):
                    pool.wait_ge(consts_in, DMA * N_CONSTS)
                for row, n, part in ((4, 0, 1), (5, 1, 1), (6, 0, 2), (7, 1, 2)):
                    if is_row(b, row):
                        subtract(0, n, part)
                after(pool, x_in[u], ahead(b, u))
                after(pool, xb_out[par], before(b, par))
                nc.gpsimd.tensor_tensor(xb[:, par], xt[:, u], bout_all[:].rearrange("p (a d) -> p a d", a=1)
                                        .broadcast_to([P, T, D]), ALU.add).then_inc(xb_made, 1)

            def subtract(b, n, part):
                after(pool, high_done if part == 1 else middle_done, 2 * b + n + 1)
                if part == 1:
                    nc.gpsimd.tensor_tensor(rest[:, n], full[:, n], split[:, n, 0, :], ALU.subtract
                                            ).then_inc(sub_done, 1)
                else:
                    nc.gpsimd.tensor_tensor(split[:, n, 2, :], rest[:, n], split[:, n, 1, :], ALU.subtract
                                            ).then_inc(sub_done, 1)

            def four_subtractions(b):
                for part in (1, 2):
                    for n in range(2):
                        subtract(b, n, part)

            def gather(b, par, nth):
                nc.gpsimd.tensor_copy(idx_now[:, par], idx_all[:, bass.ds(b * T, T)]).then_inc(idx_copied, 1)
                pool_after(idx_copied, b + 1, nth)
                for t in range(T):
                    nc.gpsimd.indirect_dma_start(xg[:, par, t, :], None, xn_rows, bass.IndirectOffsetOnAxis(
                        ap=idx_now[:, par, t:t + 1], axis=0)).then_inc(gathered[par], DMA)

            def add_expert(b, par, nth):
                for t in range(T):
                    nc.gpsimd.indirect_dma_start(out_rows, bass.IndirectOffsetOnAxis(
                        ap=idx_now[:, par, t:t + 1], axis=0), ys[:, t, :], None, compute_op=ALU.add
                    ).then_inc(added, DMA)
                    pool_after(added, DMA * 5 * b + DMA * (t + 1), nth + t)

            def add_attention(b, nth):
                pool.dma_start(out_rows[bass.ds(b * S, S), :].rearrange("(t p) d -> p t d", p=P), att[:],
                               accum_op=ALU.add).then_inc(added, DMA)
                pool_after(added, DMA * 5 * b + DMA * 5, nth)

            phase1(route_body)
            phase1(route_body, 4)
            with pool.Fori(2, B // 4) as i:
                phase1(route_body, 4 * i)
            for par in range(2):
                last = nc.gpsimd.memset(v_ones[:, par, :, :, HD:32], 1.0)
            last.then_inc(v_ones_set, 1)
            pool_after(misc_free, 6, 0)
            for par in range(2):
                pool.wait_ge(xn_out[par], DMA * B // 4)
                pool_after(xn_out[2 + par], DMA * B // 4, 2 * par + 1)
                pool_after(xb_out[par], DMA * B // 2, 2 * par + 2)
            gather(0, 0, 5)

            def body(bt):
                b, par = bt.n, bt.par
                nth = 7 + 9 * (b - 1)
                if not bt.last:
                    four_subtractions(b + 1)
                if bt.first:
                    gather(1, 1, 6)
                    return
                pool_after(misc_free, task_no(bt, "c0"), nth)
                add_expert(b - 1, 1 - par, nth + 1)
                pool_after(misc_free, task_no(bt, "o") + 1, nth + 5)
                add_attention(b - 1, nth + 6)
                if not bt.last:
                    pool_after(misc_done, task_no(bt, "c0"), nth + 7)
                    gather(b + 1, 1 - par, nth + 8)

            batches(pool, body)
            end = task_no(Batch(B - 1, 1, False, True), "y") + 1
            nth = 7 + 9 * (B - 1) - 2
            pool_after(misc_free, end, nth)
            add_expert(B - 1, 1, nth + 1)
            pool_after(misc_free, end + 1, nth + 5)
            add_attention(B - 1, nth + 6)


TOP_STEPS = 3 * (CAP // 8)
ROUTE_STEPS = 2 * (TOP_STEPS + 4)


def v_task_of_prev(bt):
    order = [n for n in TASK_AT.values()]
    if isinstance(bt.n, int) and bt.n == 1:
        return len(PROLOGUE) + order.index("v")
    return len(PROLOGUE) + len(TASK_AT) * (bt.n - 1) - 1 + order.index("v")


_INS = ['L0_attn_x', 'L0_attn_Wqkv', 'L0_attn_bqkv', 'L0_attn_Wout', 'L0_attn_bout', 'L0_ffn_router_w1',
        'L0_ffn_router_w2', 'L0_ffn_w1', 'L0_ffn_w2', 'L0_ffn_w3']


def kernel(**inputs):
    import numpy as _np
    import concourse.bacc as _bacc
    import ml_dtypes
    from concourse import mybir as _mybir
    from concourse.bass_utils import run_bass_kernel_spmd as _run

    nc = _bacc.Bacc("TRN2", target_bir_lowering=False, num_devices=1)
    arrays, args = {}, []
    for name in _INS:
        a = _np.ascontiguousarray(inputs[name])
        arrays[f"in_{name}_dram"] = a
        args.append(nc.dram_tensor(f"in_{name}_dram", a.shape, _mybir.dt.from_np(a.dtype), kind="ExternalInput").ap())
    shape = inputs['L0_attn_x'].shape
    arrays["table_dram"] = constants(shape[1])
    args.append(nc.dram_tensor("table_dram", arrays["table_dram"].shape, F32, kind="ExternalInput").ap())
    arrays["fill_dram"] = _np.repeat(_np.array([[0], [1], [1]], dtype=ml_dtypes.bfloat16), HEADS * shape[1], axis=1)
    args.append(nc.dram_tensor("fill_dram", arrays["fill_dram"].shape, BF16, kind="ExternalInput").ap())
    args.append(nc.dram_tensor("out_dram", shape, F32, kind="ExternalOutput").ap())
    attention_and_experts(nc, *args)
    r = _run(nc, [arrays], core_ids=[0])
    return r.results[0]["out_dram"]
```
